# Optimizing a Trainium2 kernel written in Bass

```python
import numpy as np
import jax
import jax.numpy as jnp

def _softmax(x, axis=-1):
    return jax.nn.softmax(x, axis=axis)

def _gelu(x):
    return jax.nn.gelu(x, approximate=True)

def _silu(x):
    return jax.nn.silu(x)

def _sigmoid(x):
    return jax.nn.sigmoid(x)

def _layernorm(x, axis=-1, eps=1e-05):
    m = jnp.mean(x, axis=axis, keepdims=True)
    v = jnp.var(x, axis=axis, keepdims=True)
    return (x - m) / jnp.sqrt(v + eps)

def _scatter_add(tgt, idx, src, axis=0):
    return tgt.at[idx].add(src)

def _segment_sum(src, seg, n):
    return jax.ops.segment_sum(src, seg, n)
kernel_name = 'mk_cond_resid_d2_seqx_r4_0ea8bd'

def setup_inputs(seed: int=0):
    np.random.seed(seed)
    _w = jnp.asarray

    def _rec_inputs():
        import jax
        import jax.numpy as jnp
        _rk = jax.random.key(seed)
        x = -0.0001538 + 1 * jax.random.normal(jax.random.fold_in(_rk, 1), (2, 1024, 256), jnp.float32)
        _lenS = 1024 - jax.random.randint(jax.random.fold_in(_rk, 7), (2,), 0, max(1, 1024 // 4) + 1, jnp.int32)
        _lenS2 = 1024 - jax.random.randint(jax.random.fold_in(_rk, 8), (2,), 0, max(1, 1024 // 4) + 1, jnp.int32)
        cond_1024 = 0.00782532 + 1.00527 * jax.random.normal(jax.random.fold_in(_rk, 11), (2, 256), jnp.float32)
        return (x, cond_1024)
    x, cond_1024 = _rec_inputs()

    def _L0_cond_setup():
        import jax, jax.numpy as jnp
        import numpy as np
        NUM_EXPERTS = 4
        TOP_K = 2
        key = jax.random.key(seed)
        ks = jax.random.split(key, 16)
        B, L, D, E, H = (8, 192, 256, NUM_EXPERTS, 1024)
        s = 0.02
        return {'context_c': jax.random.normal(ks[0], (B, L, D), jnp.float32), 'time_cond': jax.random.normal(ks[1], (B, D), jnp.float32), 'gate_w': jax.random.normal(ks[2], (3 * D, E), jnp.float32) * s, 'gate_b': jnp.zeros((E,), jnp.float32), 'time_w': jax.random.normal(ks[3], (D, 2 * E), jnp.float32) * s, 'time_b': jnp.zeros((2 * E,), jnp.float32), 'ew1': jax.random.normal(ks[4], (E, D, H), jnp.float32) * s, 'eb1': jnp.zeros((E, H), jnp.float32), 'ew2': jax.random.normal(ks[5], (E, H, D), jnp.float32) * s, 'eb2': jnp.zeros((E, D), jnp.float32), 'sw1': jax.random.normal(ks[6], (D, H), jnp.float32) * s, 'sb1': jnp.zeros((H,), jnp.float32), 'sw2': jax.random.normal(ks[7], (H, D), jnp.float32) * s, 'sb2': jnp.zeros((D,), jnp.float32)}
    _L0_cond_all = _L0_cond_setup()
    _L0_cond_in = {k: v for k, v in _L0_cond_all.items() if k in ('gate_w', 'gate_b', 'time_w', 'time_b', 'ew1', 'eb1', 'ew2', 'eb2', 'sw1', 'sb1', 'sw2', 'sb2')}
    del _L0_cond_all

    def _L1_cond_setup():
        import jax, jax.numpy as jnp
        import numpy as np
        import math
        IN_F = 256
        OUT_F = 256
        B = 16
        L = 1024
        key = jax.random.key(seed)
        k1, k2, k3 = jax.random.split(key, 3)
        Efou = jax.random.normal(k1, (B, L, IN_F), dtype=jnp.float32)
        y = jax.random.normal(k2, (B, IN_F), dtype=jnp.float32)
        weight = jax.random.normal(k3, (1, OUT_F, IN_F, 1), dtype=jnp.float32)
        return {'Efou': Efou, 'y': y, 'weight': weight}
    _L1_cond_all = _L1_cond_setup()
    _L1_cond_in = {k: v for k, v in _L1_cond_all.items() if k in ('weight',)}
    del _L1_cond_all
    return {'x': x, 'cond_1024': cond_1024, 'L0_cond_gate_w': _L0_cond_in['gate_w'], 'L0_cond_gate_b': _L0_cond_in['gate_b'], 'L0_cond_time_w': _L0_cond_in['time_w'], 'L0_cond_time_b': _L0_cond_in['time_b'], 'L0_cond_ew1': _L0_cond_in['ew1'], 'L0_cond_eb1': _L0_cond_in['eb1'], 'L0_cond_ew2': _L0_cond_in['ew2'], 'L0_cond_eb2': _L0_cond_in['eb2'], 'L0_cond_sw1': _L0_cond_in['sw1'], 'L0_cond_sb1': _L0_cond_in['sb1'], 'L0_cond_sw2': _L0_cond_in['sw2'], 'L0_cond_sb2': _L0_cond_in['sb2'], 'L1_cond_weight': _L1_cond_in['weight']}

def reference(x, cond_1024, L0_cond_gate_w, L0_cond_gate_b, L0_cond_time_w, L0_cond_time_b, L0_cond_ew1, L0_cond_eb1, L0_cond_ew2, L0_cond_eb2, L0_cond_sw1, L0_cond_sb1, L0_cond_sw2, L0_cond_sb2, L1_cond_weight):
    import jax
    import jax.numpy as jnp

    def _L0_cond_ref(context_c, time_cond, gate_w, gate_b, time_w, time_b, ew1, eb1, ew2, eb2, sw1, sb1, sw2, sb2):
        import jax, jax.numpy as jnp
        import numpy as np
        NUM_EXPERTS = 4
        TOP_K = 2
        B, L, D = context_c.shape
        E, K = (NUM_EXPERTS, TOP_K)
        L_head = L_wrist = L // 3
        head = context_c[:, :L_head]
        wrist = context_c[:, L_head:L_head + L_wrist]
        proprio = context_c[:, L_head + L_wrist:]
        full_agg = context_c.mean(axis=1)
        hp_agg = jnp.concatenate([head, proprio], axis=1).mean(axis=1)
        wp_agg = jnp.concatenate([wrist, proprio], axis=1).mean(axis=1)
        gate_in = jnp.concatenate([full_agg, hp_agg, wp_agg], axis=-1)
        gate_logits = gate_in @ gate_w + gate_b
        mod = jax.nn.silu(time_cond) @ time_w + time_b
        scale, shift = jnp.split(mod, 2, axis=-1)
        gate_logits = gate_logits * (1.0 + scale) + shift
        gate_scores = jax.nn.softmax(gate_logits, axis=-1)
        topk_w, topk_i = jax.lax.top_k(gate_scores, K)
        topk_w = topk_w / (topk_w.sum(axis=-1, keepdims=True) + 1e-08)
        onehot = (topk_i[..., None] == jnp.arange(E)[None, None, :]).astype(context_c.dtype)
        w_be = jnp.sum(topk_w[..., None] * onehot, axis=1)
        mask = np.ones((E, L), dtype=np.float32)
        mask[1, L_head:L_head + L_wrist] = 0.0
        mask[2, :L_head] = 0.0
        mask = jnp.asarray(mask)
        out = jnp.zeros_like(context_c)
        for e in range(E):
            h = jax.nn.gelu(context_c @ ew1[e] + eb1[e], approximate=True)
            y = h @ ew2[e] + eb2[e]
            out = out + w_be[:, e][:, None, None] * mask[e][None, :, None] * y
        shared = jax.nn.gelu(context_c @ sw1 + sb1, approximate=True) @ sw2 + sb2
        return out + shared

    def _L1_cond_ref(Efou, y, weight):
        import jax, jax.numpy as jnp
        import numpy as np
        import math
        IN_F = 256
        OUT_F = 256
        B = 16
        L = 1024
        b, img_size, in_f = Efou.shape
        out_f = weight.shape[1]
        scale = 1.0 / math.sqrt(in_f)
        w = scale * weight[:, :, :, 0] * y[:, None, :]
        dnorm = jax.lax.rsqrt(jnp.sum(w * w, axis=2, keepdims=True) + 1e-08)
        w = w * dnorm
        E = Efou.reshape(b, in_f, img_size)
        x = jnp.einsum('boi,bil->bol', w, E)
        return x.reshape(b, img_size, out_f)
    x = x + _L0_cond_ref(x, cond_1024, L0_cond_gate_w, L0_cond_gate_b, L0_cond_time_w, L0_cond_time_b, L0_cond_ew1, L0_cond_eb1, L0_cond_ew2, L0_cond_eb2, L0_cond_sw1, L0_cond_sb1, L0_cond_sw2, L0_cond_sb2)
    x = x + _L1_cond_ref(x, cond_1024, L1_cond_weight)
    return x

_drawn_inputs = setup_inputs


def setup_inputs(seed=0):
    import zlib

    import numpy as np

    out = dict(_drawn_inputs(seed))
    spreads = {'L0_cond_gate_b': (0.0, 2.0),
     'L0_cond_time_b': (0.0, 0.8),
     'L0_cond_eb1': (0.0, 0.367),
     'L0_cond_eb2': (0.0, 0.1),
     'L0_cond_sb1': (0.0, 0.1),
     'L0_cond_sb2': (0.0, 0.1)}
    factors = {'L0_cond_gate_w': 64.0, 'L0_cond_time_w': 5.655}
    for name, (base, spread) in spreads.items():
        noise = np.random.default_rng([zlib.crc32(name.encode()), seed]).standard_normal(out[name].shape)
        drawn = base * np.exp(spread * noise) if base else spread * noise
        out[name] = jnp.asarray(drawn.astype(out[name].dtype))
    for name, factor in factors.items():
        out[name] = (out[name] * factor).astype(out[name].dtype)
    return out
```

```python
from contextlib import ExitStack

import concourse.bass as bass
from concourse import mybir

F32 = mybir.dt.float32
F32R = mybir.dt.float32r
U32 = mybir.dt.uint32
ALU = mybir.AluOpType
ACT = mybir.ActivationFunctionType
AX_X = mybir.AxisListType.X

P = 128
EULER = 2.718281828459045
EPS_TOPK = 1e-08
EPS_NORM = 1e-08


def build(nc, x, cond, gate_w, gate_b, time_w, time_b, ew1, eb1, ew2, eb2, sw1, sb1, sw2, sb2, mod_w, out):
    B, L, D = x.shape
    E = gate_w.shape[1]
    H = sw1.shape[1]
    R = L // D
    RH = R // 2
    DC = D // P
    IC = D // P
    HC = H // P
    HALF = RH * D
    SLOTS = 2
    SEG = 3
    HEAD = L // 3
    WRIST = 2 * (L // 3)
    NOT_WRIST, NOT_HEAD = 1, 2
    GROUPS = 2 * B
    COEF = SLOTS * SEG + SEG * E
    AGG = 3
    assert HALF == 512 and B == 2 and E == 4 and DC == 2 and R == 4

    STEPS = GROUPS * (1 + SLOTS)
    LOADS = 1 + B * SLOTS

    H_RING, HID_RING, G_RING = 4, 4, 3
    LAG = 3

    USES = ["x0", "x1", "agg", "logits", "coef", "x2", "x3", "modT", "normsq",
            "T00", "M00", "T01", "M01", "T10", "M10", "T11", "M11"]
    USE = {name: n for n, name in enumerate(USES)}

    def segments(half):
        ends = [[0, -(-(HEAD - r) // R), -(-(WRIST - r) // R), D] for r in range(half * RH, half * RH + RH)]
        runs = []
        for s in range(SEG):
            spans = [(e[s], e[s + 1]) for e in ends]
            if len(set(spans)) == 1:
                runs.append((s, 0, RH, *spans[0]))
            else:
                runs += [(s, n, 1, *span) for n, span in enumerate(spans)]
        return runs

    with ExitStack() as ctx:
        def sb(name, shape, dt=F32):
            return ctx.enter_context(nc.sbuf_tensor(name, shape, dt))

        def sem(name):
            return ctx.enter_context(nc.semaphore(name))

        x_raw = sb("x_raw", [P, B, 2, IC, HALF])
        acc = sb("acc", [P, DC, GROUPS * HALF])
        x_hi = sb("x_hi", [P, DC, GROUPS * HALF], F32R)
        x_lo = sb("x_lo", [P, DC, GROUPS * HALF], F32R)
        gelu = sb("gelu", [P, G_RING, HALF])
        h_hi = sb("h_hi", [P, H_RING, HALF], F32R)
        h_lo = sb("h_lo", [P, H_RING, HALF], F32R)
        w1_raw = sb("w1_raw", [P, DC, H])
        w2_raw = sb("w2_raw", [P, HC, D])
        w1_hi = sb("w1_hi", [P, 2, DC, HC, P], F32R)
        w1_lo = sb("w1_lo", [P, 2, DC, HC, P], F32R)
        w2_hi = sb("w2_hi", [P, 2, HC, D], F32R)
        w2_lo = sb("w2_lo", [P, 2, HC, D], F32R)
        b1 = sb("b1", [P, LOADS, HC])
        eb2_col = sb("eb2_col", [P, DC, E])
        sb2_col = sb("sb2_col", [P, DC])
        agg_w = sb("agg_w", [P, R, IC, AGG])
        agg_t = sb("agg_t", [P, R, IC])
        gate_in = sb("gate_in", [P, AGG, DC, B])
        gate_w_sb = sb("gate_w_sb", [P, AGG, DC, E])
        time_w_sb = sb("time_w_sb", [P, DC, 2 * E])
        gate_b_sb = sb("gate_b_sb", [B, E])
        time_b_sb = sb("time_b_sb", [B, 2 * E])
        cond_col = sb("cond_col", [P, DC, B])
        silu_t = sb("silu_t", [P, DC, B])
        silu_e = sb("silu_e", [P, DC, B])
        silu = sb("silu", [P, DC, B])
        base_e = sb("base_e", [P, E])
        lg = sb("lg", [B, 3 * E])
        lt = sb("lt", [B, 8, E])
        prob = sb("prob", [B, 8])
        top = sb("top", [B, 8])
        top_i = sb("top_i", [B, 8], U32)
        rt = sb("rt", [B, 8, SLOTS])
        ident2 = sb("ident2", [B, B])
        iota_e = sb("iota_e", [B, E])
        seg_mask = sb("seg_mask", [B, 2, E])
        coef_row = sb("coef_row", [B, COEF])
        coef_diag = sb("coef_diag", [B, B, COEF])
        coef = sb("coef", [P, B, COEF])
        bias_t = sb("bias_t", [P, B, SEG, E])
        bias_s = sb("bias_s", [P, DC, B, SEG])
        bias = sb("bias", [P, DC, B, SEG])
        mod_raw = sb("mod_raw", [P, DC, D])
        mod_y = sb("mod_y", [P, IC, B])
        mod_t = sb("mod_t", [P, B, IC, D])
        mod_hi = sb("mod_hi", [P, B, IC, D], F32R)
        mod_lo = sb("mod_lo", [P, B, IC, D], F32R)
        mod_sq = sb("mod_sq", [P, B, IC, D])
        norm_sq = sb("norm_sq", [P, B * DC])
        minus_half = sb("minus_half", [P, B * DC])
        minus_one = sb("minus_one", [B, 1])
        norm = sb("norm", [P, B * DC])
        rows = sb("rows", [P, IC, HALF])
        rows_hi = sb("rows_hi", [P, IC, HALF], F32R)
        rows_lo = sb("rows_lo", [P, IC, HALF], F32R)
        y = sb("y", [P, DC, HALF])
        ident = sb("ident", [P, P])
        ones = sb("ones", [P, P])

        hid = [ctx.enter_context(nc.psum_tensor(f"hid{n}", [P, HALF], F32)) for n in range(HID_RING)]
        mlp = [ctx.enter_context(nc.psum_tensor(f"mlp{n}", [P, HALF], F32)) for n in range(DC)]
        extra = [ctx.enter_context(nc.psum_tensor(f"extra{n}", [P, HALF], F32)) for n in range(2)]

        x_landed = [sem(f"x_landed{g}") for g in range(GROUPS)]
        w1_landed = sem("w1_landed")
        w2_landed = sem("w2_landed")
        b1_landed = [sem(f"b1_landed{n}") for n in range(LOADS)]
        cond_landed = sem("cond_landed")
        router_landed = sem("router_landed")
        b2_landed = sem("b2_landed")
        mod_landed = sem("mod_landed")
        pool_step = sem("pool_step")
        dve_step = sem("dve_step")
        consts_ready = sem("consts_ready")
        silu_exp_ready = sem("silu_exp_ready")
        silu_ready = sem("silu_ready")
        sw_hi_ready = sem("sw_hi_ready")
        w1_ready = sem("w1_ready")
        w2_ready = sem("w2_ready")
        x_copied = sem("x_copied")
        x_ready = sem("x_ready")
        hidden_ready = sem("hidden_ready")
        gelu_ready = sem("gelu_ready")
        h_hi_ready = sem("h_hi_ready")
        h_ready = sem("h_ready")
        h_used = sem("h_used")
        acc_ready = sem("acc_ready")
        extra_ready = sem("extra_ready")
        coef_ready = sem("coef_ready")
        bias_ready = sem("bias_ready")
        mod_scaled = sem("mod_scaled")
        gate_in_ready = sem("gate_in_ready")
        logits_ready = sem("logits_ready")
        prob_ready = sem("prob_ready")
        top_ready = sem("top_ready")
        diag_ready = sem("diag_ready")
        mod_ready = sem("mod_ready")
        norm_sq_ready = sem("norm_sq_ready")
        norm_ready = sem("norm_ready")
        rows_copied = sem("rows_copied")
        rows_ready = sem("rows_ready")
        y_ready = sem("y_ready")
        stored = sem("stored")

        block = ctx.enter_context(nc.Block())

        UNITS = [(0, 0), (0, 1)] + [(1 + b * SLOTS + s, b) for b in range(B) for s in range(SLOTS)]
        LAST_STEP_OF_BUFFER = {2: 4, 3: 6, 4: 8}

        def hooks(t, j):
            return {(0, 1): ["x1"], (0, 3): ["agg"], (0, 5): ["logits"], (1, 0): ["coef"], (1, 5): ["x2"],
                    (2, 4): ["x3"], (3, 2): ["modT"], (3, 6): ["normsq"],
                    (7, 2): ["T00"], (7, 6): ["M00"], (8, 2): ["T01"], (8, 6): ["M01"],
                    (11, 2): ["T10"], (11, 6): ["M10"]}.get((t, j), [])

        TAIL = ["T11", "M11"]

        def span(g, dc=None):
            return slice(g * HALF, (g + 1) * HALF)

        w1_src = [sw1.rearrange("(c p) h -> p c h", p=P), ew1.rearrange("e (c p) h -> e p c h", p=P)]
        w2_src = [sw2.rearrange("(p j) d -> p j d", j=HC), ew2.rearrange("e (p j) d -> e p j d", j=HC)]
        b1_src = [sb1.rearrange("(p j) -> p j", j=HC), eb1.rearrange("e (p j) -> e p j", j=HC)]
        x_src = x.rearrange("b (c p f r) d -> b f p c (r d)", p=P, f=2, r=RH)
        out_dst = out.rearrange("b (c p f r) d -> b f p c (r d)", p=P, f=2, r=RH)

        @block.sync
        def _(sp):
            def load_x(g):
                sp.dma_start(x_raw[:, g // 2, g % 2], x_src[g // 2, g % 2]).then_inc(x_landed[g], 16)

            load_x(0)
            sp.dma_start(w1_raw[:], w1_src[0]).then_inc(w1_landed, 16)
            sp.dma_start(w2_raw[:], w2_src[0]).then_inc(w2_landed, 16)
            for g in range(1, GROUPS):
                load_x(g)
            sp.dma_start(mod_raw[:], mod_w[0, :, :, 0].rearrange("(c p) i -> p c i", p=P)).then_inc(mod_landed, 16)
            sp.wait_ge(top_ready, 1)
            for n in range(1, LOADS):
                b, s = (n - 1) // SLOTS, (n - 1) % SLOTS
                e = sp.value_load(top_i[b:b + 1, s:s + 1], min_val=0, max_val=E - 1)
                sp.dma_start(b1[:, n, :], b1_src[1][bass.ds(e, 1)].rearrange("e p j -> p (e j)")).then_inc(b1_landed[n], 16)
                sp.wait_ge(w1_ready, 2 * n)
                sp.dma_start(w1_raw[:], w1_src[1][bass.ds(e, 1)].rearrange("e p c h -> p (e c) h")).then_inc(w1_landed, 16)
                sp.wait_ge(w2_ready, 2 * n)
                sp.dma_start(w2_raw[:], w2_src[1][bass.ds(e, 1)].rearrange("e p j d -> p (e j) d")).then_inc(w2_landed, 16)
            for g in range(GROUPS):
                for oc in range(DC):
                    sp.wait_ge(y_ready, DC * g + oc + 1)
                    sp.dma_start(out_dst[g // 2, g % 2][:, oc], y[:, oc]).then_inc(stored, 16)
            sp.wait_ge(stored, 16 * DC * GROUPS)

        @block.gpsimd
        def _(pool):
            chain = [0]

            def link(ins):
                chain[0] += 1
                ins.then_inc(pool_step, 1)
                pool.wait_ge(pool_step, chain[0])

            g = nc.gpsimd
            g.memset(ones[:], 1.0)
            link(g.memset(ident[:], 0.0))
            link(g.affine_select(out=ident[:], in_=ident[:], compare_op=ALU.not_equal, fill=1.0, base=0,
                                 pattern=[[-1, P]], channel_multiplier=1))
            g.tensor_copy(ident2[:], ident[0:B, 0:B])
            g.memset(base_e[:], EULER)
            g.memset(minus_half[:], -0.5)
            g.memset(minus_one[:], -1.0)
            token = dict(pattern=[[1, R], [P * R, IC]], channel_multiplier=R)
            link(g.memset(agg_w[:, :, :, 0], 1.0 / L))
            link(g.memset(agg_w[:, :, :, 1], 1.0 / (L - (WRIST - HEAD))))
            link(g.affine_select(out=agg_t[:], in_=agg_w[:, :, :, 1], compare_op=ALU.is_ge, fill=0.0,
                                 base=-WRIST, **token))
            link(g.affine_select(out=agg_w[:, :, :, 2], in_=agg_w[:, :, :, 1], compare_op=ALU.is_ge, fill=0.0,
                                 base=-HEAD, **token))
            link(g.tensor_tensor(agg_w[:, :, :, 1], agg_w[:, :, :, 1], agg_w[:, :, :, 2], ALU.subtract))
            link(g.tensor_tensor(agg_w[:, :, :, 1], agg_w[:, :, :, 1], agg_t[:], ALU.add))
            for e in range(E):
                g.memset(iota_e[:, e:e + 1], float(e))
            link(g.memset(seg_mask[:], 1.0))
            g.memset(seg_mask[:, 0, NOT_HEAD:NOT_HEAD + 1], 0.0)
            g.memset(seg_mask[:, 1, NOT_WRIST:NOT_WRIST + 1], 0.0)
            g.memset(prob[:], -1.0).then_inc(consts_ready, 1)
            pool.wait_ge(consts_ready, 1)
            pool.wait_ge(cond_landed, 16 * B)
            link(g.tensor_scalar(silu_t[:], cond_col[:], -1.0, None, ALU.mult))
            flat = "p c b -> p (c b)"
            g.tensor_tensor(silu_e[:].rearrange(flat), base_e[:, 0:DC * B], silu_t[:].rearrange(flat),
                            ALU.pow).then_inc(silu_exp_ready, 1)

            pool.wait_ge(logits_ready, 1)
            pool.wait_ge(router_landed, 64)
            link(g.tensor_tensor(lt[:, 0], lg[:, 0:E], gate_b_sb[:], ALU.add))
            link(g.tensor_tensor(lt[:, 1:3], lg[:, E:3 * E].rearrange("b (a e) -> b a e", a=2),
                                 time_b_sb[:].rearrange("b (a e) -> b a e", a=2), ALU.add))
            link(g.tensor_scalar(lt[:, 3], lt[:, 1], 1.0, None, ALU.add))
            link(g.tensor_tensor(lt[:, 4], lt[:, 0], lt[:, 3], ALU.mult))
            link(g.tensor_tensor(lt[:, 4], lt[:, 4], lt[:, 2], ALU.add))
            link(g.tensor_scalar(rt[:, 0, 0:1], lt[:, 4, 0:1], lt[:, 4, 1:2], lt[:, 4, 2:3], ALU.max, ALU.max))
            link(g.tensor_scalar(rt[:, 0, 0:1], rt[:, 0, 0:1], lt[:, 4, 3:4], None, ALU.max))
            link(g.tensor_scalar(lt[:, 5], lt[:, 4], rt[:, 0, 0:1], None, ALU.subtract))
            link(g.tensor_tensor(lt[:, 6], base_e[0:B, :], lt[:, 5], ALU.pow))
            link(g.tensor_tensor(rt[:, 7], lt[:, 6, 0:2], lt[:, 6, 2:4], ALU.add))
            link(g.tensor_tensor(rt[:, 0, 1:2], rt[:, 7, 0:1], rt[:, 7, 1:2], ALU.add))
            link(g.tensor_tensor(rt[:, 0, 0:1], rt[:, 0, 1:2], minus_one[:, 0:1], ALU.pow))
            g.tensor_scalar(prob[:, 0:E], lt[:, 6], rt[:, 0, 0:1], None, ALU.mult).then_inc(prob_ready, 1)
            pool.wait_ge(top_ready, 1)
            link(g.tensor_tensor(rt[:, 1, 0:1], top[:, 0:1], top[:, 1:2], ALU.add))
            link(g.tensor_scalar(rt[:, 1, 0:1], rt[:, 1, 0:1], EPS_TOPK, None, ALU.add))
            link(g.tensor_tensor(rt[:, 1, 1:2], rt[:, 1, 0:1], minus_one[:, 0:1], ALU.pow))
            link(g.tensor_scalar(rt[:, 2], top[:, 0:SLOTS], rt[:, 1, 1:2], None, ALU.mult))
            link(g.tensor_copy(rt[:, 3], top_i[:, 0:SLOTS]))
            link(g.tensor_scalar(rt[:, 4], rt[:, 3], float(NOT_HEAD), -1.0, ALU.is_equal, ALU.mult))
            link(g.tensor_scalar(rt[:, 5], rt[:, 3], float(NOT_WRIST), -1.0, ALU.is_equal, ALU.mult))
            link(g.tensor_scalar(rt[:, 4:6], rt[:, 4:6], 1.0, None, ALU.add))
            by_slot = coef_row[:, 0:SLOTS * SEG].rearrange("b (s g) -> b s g", g=SEG)
            by_expert = coef_row[:, SLOTS * SEG:].rearrange("b (g e) -> b g e", e=E)
            g.tensor_tensor(by_slot[:, :, 0], rt[:, 2], rt[:, 4], ALU.mult)
            g.tensor_tensor(by_slot[:, :, 1], rt[:, 2], rt[:, 5], ALU.mult)
            g.tensor_copy(by_slot[:, :, 2], rt[:, 2])
            for s in range(SLOTS):
                link(g.tensor_scalar(lt[:, s], iota_e[:], rt[:, 3, s:s + 1], rt[:, 2, s:s + 1],
                                     ALU.is_equal, ALU.mult))
            link(g.tensor_tensor(by_expert[:, 2], lt[:, 0], lt[:, 1], ALU.add))
            link(g.tensor_tensor(by_expert[:, 0], by_expert[:, 2], seg_mask[:, 0], ALU.mult))
            link(g.tensor_tensor(by_expert[:, 1], by_expert[:, 2], seg_mask[:, 1], ALU.mult))
            for b in range(B):
                last = g.tensor_scalar(coef_diag[:, b], coef_row[:], ident2[:, b:b + 1], None, ALU.mult)
            last.then_inc(diag_ready, 1)

            for n in range(1, LOADS):
                if n == 2:
                    pool.wait_ge(norm_sq_ready, 1)
                    g.tensor_tensor(norm[:], norm_sq[:], minus_half[:], ALU.pow).then_inc(norm_ready, 1)
                u = n % 2
                pool.wait_ge(w1_landed, 16 * (n + 1))
                if n in LAST_STEP_OF_BUFFER:
                    pool.wait_ge(hidden_ready, HC * LAST_STEP_OF_BUFFER[n])
                src = w1_raw[:].rearrange("p c (m j) -> p c j m", j=HC)
                for c in range(DC):
                    link(g.tensor_copy(w1_hi[:, u, c], src[:, c]))
                    g.tensor_tensor(w1_lo[:, u, c], src[:, c], w1_hi[:, u, c].bitcast(F32), ALU.subtract).then_inc(w1_ready, 1)
                pool.wait_ge(w2_landed, 16 * (n + 1))
                if n in LAST_STEP_OF_BUFFER:
                    pool.wait_ge(h_used, HC * LAST_STEP_OF_BUFFER[n])
                for c in range(2):
                    js = slice(c * HC // 2, (c + 1) * HC // 2)
                    link(g.tensor_copy(w2_hi[:, u, js], w2_raw[:, js]))
                    g.tensor_tensor(w2_lo[:, u, js], w2_raw[:, js], w2_hi[:, u, js].bitcast(F32), ALU.subtract).then_inc(w2_ready, 1)

        @block.scalar
        def _(act):
            with nc.allow_non_contiguous_dma(reason="a few hundred numbers, onto partitions"):
                for b in range(B):
                    act.dma_start(cond_col[:, :, b], cond[b].rearrange("(c p) -> p c", p=P)).then_inc(cond_landed, 16)
                act.dma_start(b1[:, 0, :], b1_src[0]).then_inc(b1_landed[0], 16)
                act.dma_start(gate_w_sb[:], gate_w.rearrange("(a c p) e -> p a c e", a=AGG, p=P)).then_inc(router_landed, 16)
                act.dma_start(time_w_sb[:], time_w.rearrange("(c p) e -> p c e", p=P)).then_inc(router_landed, 16)
                act.dma_start(gate_b_sb[:], gate_b.rearrange("(a e) -> a e", a=1).to_broadcast([B, E])).then_inc(router_landed, 16)
                act.dma_start(time_b_sb[:], time_b.rearrange("(a e) -> a e", a=1).to_broadcast([B, 2 * E])).then_inc(router_landed, 16)
                act.dma_start(sb2_col[:], sb2.rearrange("(c p) -> p c", p=P)).then_inc(b2_landed, 16)
                for e in range(E):
                    act.dma_start(eb2_col[:, :, e], eb2[e].rearrange("(c p) -> p c", p=P)).then_inc(b2_landed, 16)

            w1_src_j = w1_raw[:].rearrange("p c (m j) -> p c j m", j=HC)
            act.wait_ge(w1_landed, 16)
            for q in range(2):
                js = slice(q * HC // 2, (q + 1) * HC // 2)
                for c in range(DC):
                    last = nc.scalar.activation(w1_hi[:, 0, c, js], w1_src_j[:, c, js], ACT.Copy)
                last.then_inc(sw_hi_ready, 1)

            def copy_x(grp):
                act.wait_ge(extra_ready, USE[f"x{grp}"] + 1)
                for c in range(DC):
                    nc.scalar.activation(acc[:, c, span(grp)], extra[c][:], ACT.Copy).then_inc(x_copied, 1)

            def copy_rows(name):
                act.wait_ge(extra_ready, USE[name] + 1)
                for c in range(IC):
                    nc.scalar.activation(rows[:, c], extra[c][:], ACT.Copy).then_inc(rows_copied, 1)

            copy_x(0)
            act.wait_ge(w2_landed, 16)
            for q in range(2):
                js = slice(q * HC // 2, (q + 1) * HC // 2)
                nc.scalar.activation(w2_hi[:, 0, js], w2_raw[:, js], ACT.Copy).then_inc(sw_hi_ready, 1)

            def extras(names):
                for name in names:
                    if name[0] == "x":
                        copy_x(int(name[1]))
                    elif name[0] == "T":
                        copy_rows(name)

            for t in range(STEPS):
                load = UNITS[t // 2][0]
                for j in range(HC):
                    n = HC * t + j
                    act.wait_ge(hidden_ready, n + 1)
                    if n >= G_RING:
                        act.wait_ge(h_ready, n - G_RING + 1)
                    if j == 0:
                        act.wait_ge(b1_landed[load], 16)
                    nc.scalar.activation(gelu[:, n % G_RING], hid[n % HID_RING][:], ACT.Gelu_apprx_tanh,
                                         bias=b1[:, load, j:j + 1]).then_inc(gelu_ready, 1)
                    extras(hooks(t, j))
            extras(TAIL)

        @block.vector
        def _(dve):
            chain = [0]

            def link(ins):
                chain[0] += 1
                ins.then_inc(dve_step, 1)
                dve.wait_ge(dve_step, chain[0])

            v = nc.vector

            def split_x(grp):
                for c in range(DC):
                    dve.wait_ge(x_copied, DC * grp + c + 1)
                    link(v.tensor_copy(x_hi[:, c, span(grp)], acc[:, c, span(grp)]))
                    v.tensor_tensor(x_lo[:, c, span(grp)], acc[:, c, span(grp)], x_hi[:, c, span(grp)],
                                    ALU.subtract).then_inc(x_ready, 1)

            def add_step(t):
                load, b = UNITS[t // 2]
                half = t % 2
                dve.wait_ge(h_used, HC * (t + 1))
                if t == 0:
                    dve.wait_ge(bias_ready, DC)
                g0 = (2 * b + half) * HALF
                for c in range(DC):
                    for s, r, rs, i0, i1 in segments(half):
                        to = acc[:, c, g0:g0 + HALF].rearrange("p (r i) -> p r i", r=RH)[:, r:r + rs, i0:i1]
                        of = mlp[c][:].rearrange("p (r i) -> p r i", r=RH)[:, r:r + rs, i0:i1]
                        if load == 0:
                            last = v.scalar_tensor_tensor(out=to, in0=of, scalar=bias[:, c, b, s:s + 1], in1=to,
                                                          op0=ALU.add, op1=ALU.add)
                        else:
                            k = (load - 1) % SLOTS * SEG + s
                            last = v.scalar_tensor_tensor(out=to, in0=of, scalar=coef[:, b, k:k + 1], in1=to,
                                                          op0=ALU.mult, op1=ALU.add)
                last.then_inc(acc_ready, 1)

            def extras(names):
                for name in names:
                    if name[0] == "x":
                        split_x(int(name[1]))
                        continue
                    dve.wait_ge(extra_ready, USE[name] + 1)
                    if name == "agg":
                        v.tensor_copy(gate_in[:], extra[0][:, 0:DC * B * AGG].rearrange("p (c b a) -> p a c b", c=DC, b=B)).then_inc(gate_in_ready, 1)
                    elif name == "logits":
                        v.tensor_copy(lg[:], extra[0][0:B, 0:3 * E]).then_inc(logits_ready, 1)
                    elif name == "coef":
                        v.tensor_copy(coef[:].rearrange("p b k -> p (b k)"), extra[0][:, 0:B * COEF]).then_inc(coef_ready, 1)
                        dve.wait_ge(coef_ready, 1)
                        dve.wait_ge(b2_landed, 16 * (1 + E))
                        for c in range(DC):
                            link(v.tensor_tensor(bias_t[:], coef[:, :, SLOTS * SEG:].rearrange("p b (g e) -> p b g e", e=E),
                                                 eb2_col[:, c, :].unsqueeze(1).unsqueeze(1).to_broadcast([P, B, SEG, E]), ALU.mult))
                            link(v.tensor_reduce(bias_s[:, c], bias_t[:], AX_X, ALU.add))
                            v.tensor_scalar(bias[:, c], bias_s[:, c], sb2_col[:, c:c + 1], None, ALU.add).then_inc(bias_ready, 1)
                    elif name == "modT":
                        dve.wait_ge(cond_landed, 16 * B)
                        link(v.tensor_scalar(mod_y[:], cond_col[:], float(D) ** -0.5, None, ALU.mult))
                        for b in range(B):
                            for c in range(IC):
                                v.tensor_scalar(mod_t[:, b, c], extra[0][:, c * D:(c + 1) * D], mod_y[:, c, b:b + 1],
                                                None, ALU.mult).then_inc(mod_scaled, 1)
                        dve.wait_ge(mod_scaled, B * IC)
                        v.tensor_tensor(mod_sq[:], mod_t[:], mod_t[:], ALU.mult).then_inc(mod_ready, 1)
                        v.tensor_copy(mod_hi[:], mod_t[:]).then_inc(mod_ready, 1)
                        dve.wait_ge(mod_ready, 2)
                        v.tensor_tensor(mod_lo[:], mod_t[:], mod_hi[:], ALU.subtract).then_inc(mod_ready, 1)
                    elif name == "normsq":
                        v.tensor_scalar(norm_sq[:], extra[0][:, 0:B * DC], EPS_NORM, None, ALU.add).then_inc(norm_sq_ready, 1)
                    elif name[0] == "T":
                        f = 2 * int(name[1]) + int(name[2])
                        for c in range(IC):
                            dve.wait_ge(rows_copied, IC * f + c + 1)
                            link(v.tensor_copy(rows_hi[:, c], rows[:, c]))
                            v.tensor_tensor(rows_lo[:, c], rows[:, c], rows_hi[:, c], ALU.subtract).then_inc(rows_ready, 1)
                    elif name[0] == "M":
                        b, f = int(name[1]), 2 * int(name[1]) + int(name[2])
                        dve.wait_ge(norm_ready, 1)
                        for c in range(DC):
                            if f > 0:
                                dve.wait_ge(stored, 16 * DC * f)
                            v.scalar_tensor_tensor(out=y[:, c], in0=extra[c][:], scalar=norm[:, b * DC + c:b * DC + c + 1],
                                                   in1=rows[:, c], op0=ALU.mult, op1=ALU.add).then_inc(y_ready, 1)

            dve.wait_ge(silu_exp_ready, 1)
            link(v.tensor_scalar(silu_t[:], silu_e[:], 1.0, None, ALU.add))
            link(v.reciprocal(silu_e[:], silu_t[:]))
            v.tensor_tensor(silu[:], silu_e[:], cond_col[:], ALU.mult).then_inc(silu_ready, 1)

            w1_src_j = w1_raw[:].rearrange("p c (m j) -> p c j m", j=HC)
            for q in range(2):
                js = slice(q * HC // 2, (q + 1) * HC // 2)
                dve.wait_ge(sw_hi_ready, q + 1)
                for c in range(DC):
                    last = v.tensor_tensor(w1_lo[:, 0, c, js], w1_src_j[:, c, js], w1_hi[:, 0, c, js], ALU.subtract)
                last.then_inc(w1_ready, 1)
            split_x(0)
            for q in range(2):
                js = slice(q * HC // 2, (q + 1) * HC // 2)
                dve.wait_ge(sw_hi_ready, 2 + q + 1)
                v.tensor_tensor(w2_lo[:, 0, js], w2_raw[:, js], w2_hi[:, 0, js], ALU.subtract).then_inc(w2_ready, 1)

            for t in range(STEPS):
                if t == 1:
                    extras(["coef"])
                if t > 0:
                    add_step(t - 1)
                for j in range(HC):
                    n = HC * t + j
                    if n >= H_RING:
                        dve.wait_ge(h_used, n - H_RING + 1)
                    dve.wait_ge(gelu_ready, n + 1)
                    v.tensor_copy(h_hi[:, n % H_RING], gelu[:, n % G_RING]).then_inc(h_hi_ready, 1)
                    dve.wait_ge(h_hi_ready, n + 1)
                    v.tensor_tensor(h_lo[:, n % H_RING], gelu[:, n % G_RING], h_hi[:, n % H_RING],
                                    ALU.subtract).then_inc(h_ready, 1)
                    extras([name for name in hooks(t, j) if name != "coef"])
                    if (t, j) == (0, HC - 1):
                        dve.wait_ge(prob_ready, 1)
                        v.max(top[:], prob[:]).then_inc(dve_step, 1)
                        chain[0] += 1
                        dve.wait_ge(dve_step, chain[0])
                        v.max_index(top_i[:], top[:], prob[:]).then_inc(top_ready, 1)
            add_step(STEPS - 1)
            extras(TAIL)

        @block.tensor
        def _(pe):
            def product(to, pairs):
                last = len(pairs) - 1
                for k, ((s_hi, s_lo), (m_hi, m_lo)) in enumerate(pairs):
                    nc.tensor.matmul(to, s_hi, m_hi, start=(k == 0), stop=False)
                    nc.tensor.matmul(to, s_hi, m_lo, start=False, stop=False)
                    ins = nc.tensor.matmul(to, s_lo, m_hi, start=False, stop=(k == last))
                return ins

            def free_extra(name):
                k = USE[name]
                if k == 0:
                    return
                was = USES[k - 1]
                if was[0] == "x":
                    pe.wait_ge(x_copied, DC * (int(was[1]) + 1))
                elif was[0] == "T":
                    pe.wait_ge(rows_copied, IC * (2 * int(was[1]) + int(was[2]) + 1))
                elif was[0] == "M":
                    pe.wait_ge(y_ready, DC * (2 * int(was[1]) + int(was[2]) + 1))
                elif was == "modT":
                    pe.wait_ge(mod_scaled, B * IC)
                else:
                    pe.wait_ge({"agg": gate_in_ready, "logits": logits_ready, "coef": coef_ready,
                                "normsq": norm_sq_ready}[was], 1)

            def extras(names):
                for name in names:
                    free_extra(name)
                    if name[0] == "x":
                        grp = int(name[1])
                        pe.wait_ge(x_landed[grp], 16)
                        for c in range(DC):
                            for r in range(RH):
                                for i in range(IC):
                                    k = (r * IC + i) * P
                                    last = nc.tensor.transpose(extra[c][:, k:k + P],
                                                               x_raw[:, grp // 2, grp % 2, i, r * D + c * P:r * D + (c + 1) * P], ident[:])
                    elif name == "agg":
                        for grp in range(GROUPS):
                            pe.wait_ge(x_landed[grp], 16)
                        for c in range(DC):
                            for b in range(B):
                                k = (c * B + b) * AGG
                                n = 0
                                for r in range(R):
                                    for i in range(IC):
                                        n += 1
                                        last = nc.tensor.matmul(extra[0][:, k:k + AGG],
                                                                x_raw[:, b, r // RH, i, r % RH * D + c * P:r % RH * D + (c + 1) * P],
                                                                agg_w[:, r, i], start=(n == 1), stop=(n == R * IC))
                    elif name == "logits":
                        pe.wait_ge(gate_in_ready, 1)
                        pe.wait_ge(router_landed, 64)
                        pe.wait_ge(silu_ready, 1)
                        for a in range(AGG):
                            for c in range(DC):
                                nc.tensor.matmul(extra[0][0:B, 0:E], gate_in[:, a, c], gate_w_sb[:, a, c],
                                                 start=(a + c == 0), stop=(a == AGG - 1 and c == DC - 1))
                        for c in range(DC):
                            last = nc.tensor.matmul(extra[0][0:B, E:3 * E], silu[:, c], time_w_sb[:, c],
                                                    start=(c == 0), stop=(c == DC - 1))
                    elif name == "coef":
                        pe.wait_ge(diag_ready, 1)
                        last = nc.tensor.matmul(extra[0][:, 0:B * COEF], ones[0:B, :],
                                                coef_diag[:].rearrange("b c k -> b (c k)"), start=True, stop=True)
                    elif name == "modT":
                        pe.wait_ge(mod_landed, 16)
                        for i in range(IC):
                            for o in range(DC):
                                k = i * D + o * P
                                last = nc.tensor.transpose(extra[0][:, k:k + P], mod_raw[:, o, i * P:(i + 1) * P], ident[:])
                    elif name == "normsq":
                        pe.wait_ge(mod_ready, 1)
                        for b in range(B):
                            for o in range(DC):
                                k = b * DC + o
                                for i in range(IC):
                                    last = nc.tensor.matmul(extra[0][:, k:k + 1], mod_sq[:, b, i, o * P:(o + 1) * P],
                                                            ones[:, 0:1], start=(i == 0), stop=(i == IC - 1))
                    elif name[0] == "T":
                        b, f = int(name[1]), int(name[2])
                        pe.wait_ge(acc_ready, 2 * (SLOTS * b + SLOTS + B - 1) + f + 1)
                        for i in range(IC):
                            for r in range(RH):
                                for c in range(DC):
                                    k = (2 * b + f) * HALF + r * D + i * P
                                    last = nc.tensor.transpose(extra[i][:, r * D + c * P:r * D + (c + 1) * P],
                                                               acc[:, c, k:k + P], ident[:])
                    elif name[0] == "M":
                        b, f = int(name[1]), int(name[2])
                        pe.wait_ge(rows_ready, IC * (2 * b + f + 1))
                        pe.wait_ge(mod_ready, 3)
                        for o in range(DC):
                            os = slice(o * P, (o + 1) * P)
                            last = product(extra[o][:], [((mod_hi[:, b, i, os], mod_lo[:, b, i, os]), (rows_hi[:, i], rows_lo[:, i]))
                                                         for i in range(IC)])
                    last.then_inc(extra_ready, 1)

            pe.wait_ge(consts_ready, 1)
            extras(["x0"])
            for t in range(STEPS):
                load, b = UNITS[t // 2]
                grp = 2 * b + t % 2
                u = load % 2

                def first(j):
                    n = HC * t + j
                    if j == 0:
                        pe.wait_ge(x_ready, DC * (grp + 1))
                    if load == 0 and j in (0, HC // 2):
                        pe.wait_ge(w1_ready, 1 + j // (HC // 2))
                    elif load and j == 0:
                        pe.wait_ge(w1_ready, 2 * (load + 1))
                    if n >= HID_RING:
                        pe.wait_ge(gelu_ready, n - HID_RING + 1)
                    product(hid[n % HID_RING][:], [((w1_hi[:, u, c, j], w1_lo[:, u, c, j]),
                                                    (x_hi[:, c, span(grp)], x_lo[:, c, span(grp)]))
                                                   for c in range(DC)]).then_inc(hidden_ready, 1)

                def second(j):
                    n = HC * t + j
                    if load == 0 and j in (0, HC // 2):
                        pe.wait_ge(w2_ready, 1 + j // (HC // 2))
                    elif load and j == 0:
                        pe.wait_ge(w2_ready, 2 * (load + 1))
                    if j == 0 and t > 0:
                        pe.wait_ge(acc_ready, t)
                    pe.wait_ge(h_ready, n + 1)
                    q = n % HID_RING
                    for c in range(DC):
                        cs = slice(c * P, (c + 1) * P)
                        nc.tensor.matmul(mlp[c][:], w2_hi[:, u, j, cs], h_hi[:, q], start=(j == 0), stop=False)
                        nc.tensor.matmul(mlp[c][:], w2_hi[:, u, j, cs], h_lo[:, q], start=False, stop=False)
                        last = nc.tensor.matmul(mlp[c][:], w2_lo[:, u, j, cs], h_hi[:, q], start=False, stop=(j == HC - 1))
                    last.then_inc(h_used, 1)

                for j in range(HC):
                    first(j)
                    extras(hooks(t, j))
                    if j >= LAG:
                        second(j - LAG)
                for j in range(HC - LAG, HC):
                    second(j)
            extras(TAIL)


_INS = ['x', 'cond_1024', 'L0_cond_gate_w', 'L0_cond_gate_b', 'L0_cond_time_w', 'L0_cond_time_b',
        'L0_cond_ew1', 'L0_cond_eb1', 'L0_cond_ew2', 'L0_cond_eb2', 'L0_cond_sw1', 'L0_cond_sb1',
        'L0_cond_sw2', 'L0_cond_sb2', 'L1_cond_weight']
_OUTS = [((2, 1024, 256), 'float32')]


def kernel(**inputs):
    import numpy as _np
    import concourse.bacc as _bacc
    from concourse import mybir as _mybir
    from concourse.bass_utils import run_bass_kernel_spmd as _run

    nc = _bacc.Bacc("TRN2", target_bir_lowering=False, num_devices=1)
    arrays, args = {}, []
    for name in _INS:
        a = _np.ascontiguousarray(inputs[name])
        arrays[f"in_{name}_dram"] = a
        args.append(nc.dram_tensor(f"in_{name}_dram", a.shape, _mybir.dt.from_np(a.dtype), kind="ExternalInput").ap())
    for i, (shape, dtype) in enumerate(_OUTS):
        dt = _mybir.dt.from_np(_np.dtype(dtype))
        args.append(nc.dram_tensor(f"out_{i}_dram", shape, dt, kind="ExternalOutput").ap())
    build(nc, *args)
    r = _run(nc, [arrays], core_ids=[0])
    return r.results[0]["out_0_dram"]
```

```python
from contextlib import ExitStack

import concourse.bass as bass
from concourse import mybir

F32 = mybir.dt.float32
F32R = mybir.dt.float32r
U32 = mybir.dt.uint32
ALU = mybir.AluOpType
ACT = mybir.ActivationFunctionType
AX_X = mybir.AxisListType.X

P = 128
EULER = 2.718281828459045
EPS_TOPK = 1e-08
EPS_NORM = 1e-08


def build(nc, x, cond, gate_w, gate_b, time_w, time_b, ew1, eb1, ew2, eb2, sw1, sb1, sw2, sb2, mod_w, out):
    B, L, D = x.shape
    E = gate_w.shape[1]
    H = sw1.shape[1]
    R = L // D
    RH = R // 2
    DC = D // P
    IC = D // P
    HC = H // P
    HALF = RH * D
    SLOTS = 2
    SEG = 3
    HEAD = L // 3
    WRIST = 2 * (L // 3)
    NOT_WRIST, NOT_HEAD = 1, 2
    GROUPS = 2 * B
    COEF = SLOTS * SEG + SEG * E
    AGG = 3
    assert HALF == 512 and B == 2 and E == 4 and DC == 2 and R == 4

    STEPS = GROUPS * (1 + SLOTS)
    LOADS = 1 + B * SLOTS

    H_RING, HID_RING, G_RING = 4, 4, 3
    LAG = 3

    USES = ["x0", "x1", "x2", "x3", "logits", "coef", "modT", "normsq",
            "T00", "M00", "T01", "M01", "T10", "M10", "T11", "M11"]
    USE = {name: n for n, name in enumerate(USES)}

    head_i, wrist_i = -(-HEAD // R), WRIST // R
    from_i = HEAD // R - (D - HEAD // R) % 2
    ALL = [(0, D)]
    WINDOWS = {None: ALL, NOT_WRIST: [(0, head_i), (wrist_i, D)], NOT_HEAD: [(from_i, D)]}
    assert head_i == D - wrist_i and head_i % 2 == 0

    def width(windows):
        return RH * sum(b - a for a, b in windows)

    def pieces(half, windows=ALL):
        found = []
        for s in range(SEG):
            by_r = []
            for r in range(half * RH, half * RH + RH):
                ends = [0, -(-(HEAD - r) // R), -(-(WRIST - r) // R), D]
                row, at = [], 0
                for a, b in windows:
                    i0, i1 = max(a, ends[s]), min(b, ends[s + 1])
                    if i0 < i1:
                        row.append((i0, i1, at + i0 - a))
                    at += b - a
                by_r.append(row)
            if all(row == by_r[0] for row in by_r):
                found += [(s, 0, RH, *run) for run in by_r[0]]
            else:
                found += [(s, r, 1, *run) for r, row in enumerate(by_r) for run in row]
        return found

    with ExitStack() as ctx:
        def sb(name, shape, dt=F32):
            return ctx.enter_context(nc.sbuf_tensor(name, shape, dt))

        def sem(name):
            return ctx.enter_context(nc.semaphore(name))

        x_raw = sb("x_raw", [P, B, 2, IC, HALF])
        acc = sb("acc", [P, DC, GROUPS * HALF])
        x_hi = sb("x_hi", [P, DC, GROUPS * HALF], F32R)
        x_lo = sb("x_lo", [P, DC, GROUPS * HALF], F32R)
        gelu = sb("gelu", [P, G_RING, HALF])
        h_hi = sb("h_hi", [P, H_RING, HALF], F32R)
        h_lo = sb("h_lo", [P, H_RING, HALF], F32R)
        w1_raw = sb("w1_raw", [P, DC, H])
        w2_raw = sb("w2_raw", [P, HC, D])
        w1_hi = sb("w1_hi", [P, 2, DC, HC, P], F32R)
        w1_lo = sb("w1_lo", [P, 2, DC, HC, P], F32R)
        w2_hi = sb("w2_hi", [P, 2, HC, D], F32R)
        w2_lo = sb("w2_lo", [P, 2, HC, D], F32R)
        b1 = sb("b1", [P, LOADS, HC])
        eb2_col = sb("eb2_col", [P, DC, E])
        sb2_col = sb("sb2_col", [P, DC])
        RUNS = 3
        run_sum = sb("run_sum", [P, SEG, DC, B, RUNS])
        seg_sum = sb("seg_sum", [P, SEG, DC, B])
        avg_w = sb("avg_w", [P, AGG, DC, E])
        seg_w = sb("seg_w", [P, SEG, DC, E])
        gate_w_sb = sb("gate_w_sb", [P, AGG, DC, E])
        time_w_sb = sb("time_w_sb", [P, DC, 2 * E])
        gate_b_sb = sb("gate_b_sb", [B, E])
        time_b_sb = sb("time_b_sb", [B, 2 * E])
        cond_col = sb("cond_col", [P, DC, B])
        silu_t = sb("silu_t", [P, DC, B])
        silu_e = sb("silu_e", [P, DC, B])
        silu = sb("silu", [P, DC, B])
        base_e = sb("base_e", [P, E])
        lg = sb("lg", [B, 3 * E])
        lt = sb("lt", [B, 8, E])
        prob = sb("prob", [B, 8])
        top = sb("top", [B, 8])
        top_i = sb("top_i", [B, 8], U32)
        rt = sb("rt", [B, 8, SLOTS])
        ident2 = sb("ident2", [B, B])
        iota_e = sb("iota_e", [B, E])
        seg_mask = sb("seg_mask", [B, 2, E])
        coef_row = sb("coef_row", [B, COEF])
        coef_diag = sb("coef_diag", [B, B, COEF])
        coef = sb("coef", [P, B, COEF])
        bias_t = sb("bias_t", [P, B, SEG, E])
        bias = sb("bias", [P, DC, B, SEG])
        mod_raw = sb("mod_raw", [P, DC, D])
        mod_y = sb("mod_y", [P, IC, B])
        mod_t = sb("mod_t", [P, B, IC, D])
        mod_hi = sb("mod_hi", [P, B, IC, D], F32R)
        mod_lo = sb("mod_lo", [P, B, IC, D], F32R)
        mod_sq = sb("mod_sq", [P, B, IC, D])
        norm_sq = sb("norm_sq", [P, B * DC])
        minus_half = sb("minus_half", [P, B * DC])
        minus_one = sb("minus_one", [B, 1])
        norm = sb("norm", [P, B * DC])
        rows = sb("rows", [P, IC, HALF])
        rows_hi = sb("rows_hi", [P, IC, HALF], F32R)
        rows_lo = sb("rows_lo", [P, IC, HALF], F32R)
        y = sb("y", [P, DC, HALF])
        ident = sb("ident", [P, P])
        table_warm = sb("table_warm", [P, 1])
        ones = sb("ones", [P, P])

        hid = [ctx.enter_context(nc.psum_tensor(f"hid{n}", [P, HALF], F32)) for n in range(HID_RING)]
        mlp = [ctx.enter_context(nc.psum_tensor(f"mlp{n}", [P, HALF], F32)) for n in range(DC)]
        extra = [ctx.enter_context(nc.psum_tensor(f"extra{n}", [P, HALF], F32)) for n in range(2)]

        x_landed = [sem(f"x_landed{g}") for g in range(GROUPS)]
        w1_landed = sem("w1_landed")
        w2_landed = sem("w2_landed")
        b1_landed = [sem(f"b1_landed{n}") for n in range(LOADS)]
        cond_landed = sem("cond_landed")
        router_landed = sem("router_landed")
        b2_landed = sem("b2_landed")
        mod_landed = sem("mod_landed")
        pool_step = sem("pool_step")
        dve_step = sem("dve_step")
        consts_ready = sem("consts_ready")
        silu_exp_ready = sem("silu_exp_ready")
        silu_ready = sem("silu_ready")
        sw_hi_ready = sem("sw_hi_ready")
        w1_ready = sem("w1_ready")
        w2_ready = sem("w2_ready")
        x_copied = sem("x_copied")
        x_ready = [sem(f"x_ready{g}") for g in range(GROUPS)]
        sw1_landed = [sem(f"sw1_landed{c}") for c in range(DC)]
        ident_ready = sem("ident_ready")
        seg_w_ready = sem("seg_w_ready")
        seg_sum_ready = sem("seg_sum_ready")
        rows_in_psum = sem("rows_in_psum")
        conv_ready = sem("conv_ready")
        hidden_ready = sem("hidden_ready")
        gelu_ready = sem("gelu_ready")
        h_hi_ready = sem("h_hi_ready")
        h_ready = sem("h_ready")
        step_ready = sem("step_ready")
        h_used = sem("h_used")
        acc_ready = sem("acc_ready")
        extra_ready = sem("extra_ready")
        coef_ready = sem("coef_ready")
        bias_ready = sem("bias_ready")
        biases_added = sem("biases_added")
        mod_scaled = sem("mod_scaled")
        logits_ready = sem("logits_ready")
        prob_ready = sem("prob_ready")
        top_ready = sem("top_ready")
        diag_ready = sem("diag_ready")
        mod_ready = sem("mod_ready")
        norm_sq_ready = sem("norm_sq_ready")
        norm_ready = sem("norm_ready")
        rows_copied = sem("rows_copied")
        rows_ready = sem("rows_ready")
        y_ready = sem("y_ready")
        stored = sem("stored")

        block = ctx.enter_context(nc.Block())

        UNITS = [(0, 0), (0, 1)] + [(1 + b * SLOTS + s, b) for b in range(B) for s in range(SLOTS)]
        LAST_STEP_OF_BUFFER = {2: 4, 3: 6, 4: 8}

        def hooks(t, j):
            return {(0, 0): ["x1", "sum0"], (0, 2): ["x2", "sum1"], (0, 3): ["x3", "sum2"],
                    (0, 4): ["sum3"], (0, 6): ["logits"], (1, 3): ["coef"], (3, 2): ["modT"], (3, 6): ["normsq"],
                    (7, 2): ["T00"], (7, 6): ["M00"], (8, 2): ["T01"], (8, 6): ["M01"],
                    (11, 2): ["T10"], (11, 6): ["M10"]}.get((t, j), [])

        TAIL = ["T11", "M11"]

        def span(g):
            return slice(g * HALF, (g + 1) * HALF)

        def columns(tile, c, g, windows):
            whole = tile[:, c, span(g)]
            if len(windows) == 2:
                (_, a), (b, _) = windows
                return bass.AP(whole.tensor, whole.offset, [list(whole.ap[0]), [D, RH], [b, 2], [1, a]])
            (a, b), = windows
            return whole.rearrange("p (r i) -> p r i", r=RH)[:, :, a:b]

        def load_experts(eng):
            eng.wait_ge(top_ready, 1)
            return [eng.value_load(top_i[b:b + 1, s:s + 1], min_val=0, max_val=E - 1)
                    for b in range(B) for s in range(SLOTS)]

        def by_expert_kind(eng, expert, body):
            with eng.If(expert == NOT_WRIST):
                body(NOT_WRIST)
            with eng.Else():
                with eng.If(expert == NOT_HEAD):
                    body(NOT_HEAD)
                with eng.Else():
                    body(None)
                eng.nop()

        w1_src = [sw1.rearrange("(c p) h -> p c h", p=P), ew1.rearrange("e (c p) h -> e p c h", p=P)]
        w2_src = [sw2.rearrange("(p j) d -> p j d", j=HC), ew2.rearrange("e (p j) d -> e p j d", j=HC)]
        b1_src = [sb1.rearrange("(p j) -> p j", j=HC), eb1.rearrange("e (p j) -> e p j", j=HC)]
        x_src = x.rearrange("b (c p f r) d -> b f p c (r d)", p=P, f=2, r=RH)
        out_dst = out.rearrange("b (c p f r) d -> b f p c (r d)", p=P, f=2, r=RH)

        @block.sync
        def _(sp):
            def load_x(g):
                sp.dma_start(x_raw[:, g // 2, g % 2], x_src[g // 2, g % 2]).then_inc(x_landed[g], 16)

            load_x(0)
            for c in range(DC):
                sp.dma_start(w1_raw[:, c], w1_src[0][:, c]).then_inc(sw1_landed[c], 16)
            sp.dma_start(b1[:, 0, :], b1_src[0]).then_inc(b1_landed[0], 16)
            sp.dma_start(w2_raw[:], w2_src[0]).then_inc(w2_landed, 16)
            for g in range(1, GROUPS):
                load_x(g)
            with nc.allow_non_contiguous_dma(reason="a few hundred numbers, onto partitions"):
                for b in range(B):
                    sp.dma_start(cond_col[:, :, b], cond[b].rearrange("(c p) -> p c", p=P)).then_inc(cond_landed, 16)
                sp.dma_start(gate_w_sb[:], gate_w.rearrange("(a c p) e -> p a c e", a=AGG, p=P)).then_inc(router_landed, 16)
                sp.dma_start(time_w_sb[:], time_w.rearrange("(c p) e -> p c e", p=P)).then_inc(router_landed, 16)
                sp.dma_start(gate_b_sb[:], gate_b.rearrange("(a e) -> a e", a=1).to_broadcast([B, E])).then_inc(router_landed, 16)
                sp.dma_start(time_b_sb[:], time_b.rearrange("(a e) -> a e", a=1).to_broadcast([B, 2 * E])).then_inc(router_landed, 16)
                sp.dma_start(sb2_col[:], sb2.rearrange("(c p) -> p c", p=P)).then_inc(b2_landed, 16)
                for e in range(E):
                    sp.dma_start(eb2_col[:, :, e], eb2[e].rearrange("(c p) -> p c", p=P)).then_inc(b2_landed, 16)
            sp.dma_start(mod_raw[:], mod_w[0, :, :, 0].rearrange("(c p) i -> p c i", p=P)).then_inc(mod_landed, 16)
            experts = load_experts(sp)
            for n in range(1, LOADS):
                e = experts[n - 1]
                sp.dma_start(b1[:, n, :], b1_src[1][bass.ds(e, 1)].rearrange("e p j -> p (e j)")).then_inc(b1_landed[n], 16)
                sp.wait_ge(w1_ready, 2 * DC + 2 * (n - 1))
                sp.dma_start(w1_raw[:], w1_src[1][bass.ds(e, 1)].rearrange("e p c h -> p (e c) h")).then_inc(w1_landed, 16)
                sp.wait_ge(w2_ready, 2 * n)
                sp.dma_start(w2_raw[:], w2_src[1][bass.ds(e, 1)].rearrange("e p j d -> p (e j) d")).then_inc(w2_landed, 16)
            for g in range(GROUPS):
                for oc in range(DC):
                    sp.wait_ge(y_ready, DC * g + oc + 1)
                    sp.dma_start(out_dst[g // 2, g % 2][:, oc], y[:, oc]).then_inc(stored, 16)
            sp.wait_ge(stored, 16 * DC * GROUPS)

        @block.gpsimd
        def _(pool):
            chain = [0]

            def link(ins):
                chain[0] += 1
                ins.then_inc(pool_step, 1)
                pool.wait_ge(pool_step, chain[0])

            g = nc.gpsimd
            link(g.memset(ident[:], 0.0))
            g.affine_select(out=ident[:], in_=ident[:], compare_op=ALU.not_equal, fill=1.0, base=0,
                            pattern=[[-1, P]], channel_multiplier=1).then_inc(ident_ready, 1)
            pool.wait_ge(ident_ready, 1)
            g.memset(ones[:], 1.0)
            g.tensor_copy(ident2[:], ident[0:B, 0:B])
            g.memset(base_e[:], EULER)
            g.memset(minus_half[:], -0.5)
            g.memset(minus_one[:], -1.0)
            for e in range(E):
                g.memset(iota_e[:, e:e + 1], float(e))
            link(g.memset(seg_mask[:], 1.0))
            g.memset(seg_mask[:, 0, NOT_HEAD:NOT_HEAD + 1], 0.0)
            g.memset(seg_mask[:, 1, NOT_WRIST:NOT_WRIST + 1], 0.0)
            g.memset(prob[:], -1.0).then_inc(consts_ready, 1)
            pool.wait_ge(consts_ready, 1)
            pool.wait_ge(cond_landed, 16 * B)
            link(g.tensor_scalar(silu_t[:], cond_col[:], -1.0, None, ALU.mult))
            flat = "p c b -> p (c b)"
            g.tensor_tensor(silu_e[:].rearrange(flat), base_e[:, 0:DC * B], silu_t[:].rearrange(flat),
                            ALU.pow).then_inc(silu_exp_ready, 1)

            pool.wait_ge(router_landed, 64)
            for a, tokens in enumerate((L, L - (WRIST - HEAD), L - HEAD)):
                last = g.tensor_scalar(avg_w[:, a], gate_w_sb[:, a], 1.0 / tokens, None, ALU.mult)
            link(last)
            link(g.tensor_tensor(seg_w[:, 0], avg_w[:, 0], avg_w[:, 1], ALU.add))
            g.tensor_tensor(seg_w[:, 1], avg_w[:, 0], avg_w[:, 2], ALU.add)
            g.tensor_tensor(seg_w[:, 2], seg_w[:, 0], avg_w[:, 2], ALU.add).then_inc(seg_w_ready, 1)
            for grp in range(1, GROUPS):
                pool.wait_ge(x_copied, DC * (grp + 1))
                for c in range(DC):
                    g.tensor_tensor(x_lo[:, c, span(grp)], acc[:, c, span(grp)], x_hi[:, c, span(grp)],
                                    ALU.subtract).then_inc(x_ready[grp], 1)
            pool.wait_ge(logits_ready, 1)
            link(g.tensor_tensor(lt[:, 0], lg[:, 0:E], gate_b_sb[:], ALU.add))
            link(g.tensor_tensor(lt[:, 1:3], lg[:, E:3 * E].rearrange("b (a e) -> b a e", a=2),
                                 time_b_sb[:].rearrange("b (a e) -> b a e", a=2), ALU.add))
            link(g.tensor_scalar(lt[:, 3], lt[:, 1], 1.0, None, ALU.add))
            link(g.tensor_tensor(lt[:, 4], lt[:, 0], lt[:, 3], ALU.mult))
            link(g.tensor_tensor(lt[:, 4], lt[:, 4], lt[:, 2], ALU.add))
            link(g.tensor_scalar(rt[:, 0, 0:1], lt[:, 4, 0:1], lt[:, 4, 1:2], lt[:, 4, 2:3], ALU.max, ALU.max))
            link(g.tensor_scalar(rt[:, 0, 0:1], rt[:, 0, 0:1], lt[:, 4, 3:4], None, ALU.max))
            link(g.tensor_scalar(lt[:, 5], lt[:, 4], rt[:, 0, 0:1], None, ALU.subtract))
            link(g.tensor_tensor(lt[:, 6], base_e[0:B, :], lt[:, 5], ALU.pow))
            link(g.tensor_tensor(rt[:, 7], lt[:, 6, 0:2], lt[:, 6, 2:4], ALU.add))
            link(g.tensor_tensor(rt[:, 0, 1:2], rt[:, 7, 0:1], rt[:, 7, 1:2], ALU.add))
            link(g.tensor_tensor(rt[:, 0, 0:1], rt[:, 0, 1:2], minus_one[:, 0:1], ALU.pow))
            g.tensor_scalar(prob[:, 0:E], lt[:, 6], rt[:, 0, 0:1], None, ALU.mult).then_inc(prob_ready, 1)
            pool.wait_ge(top_ready, 1)
            link(g.tensor_tensor(rt[:, 1, 0:1], top[:, 0:1], top[:, 1:2], ALU.add))
            link(g.tensor_scalar(rt[:, 1, 0:1], rt[:, 1, 0:1], EPS_TOPK, None, ALU.add))
            link(g.tensor_tensor(rt[:, 1, 1:2], rt[:, 1, 0:1], minus_one[:, 0:1], ALU.pow))
            link(g.tensor_scalar(rt[:, 2], top[:, 0:SLOTS], rt[:, 1, 1:2], None, ALU.mult))
            link(g.tensor_copy(rt[:, 3], top_i[:, 0:SLOTS]))
            link(g.tensor_scalar(rt[:, 4], rt[:, 3], float(NOT_HEAD), -1.0, ALU.is_equal, ALU.mult))
            link(g.tensor_scalar(rt[:, 5], rt[:, 3], float(NOT_WRIST), -1.0, ALU.is_equal, ALU.mult))
            link(g.tensor_scalar(rt[:, 4:6], rt[:, 4:6], 1.0, None, ALU.add))
            by_slot = coef_row[:, 0:SLOTS * SEG].rearrange("b (s g) -> b s g", g=SEG)
            by_expert = coef_row[:, SLOTS * SEG:].rearrange("b (g e) -> b g e", e=E)
            g.tensor_tensor(by_slot[:, :, 0], rt[:, 2], rt[:, 4], ALU.mult)
            g.tensor_tensor(by_slot[:, :, 1], rt[:, 2], rt[:, 5], ALU.mult)
            g.tensor_copy(by_slot[:, :, 2], rt[:, 2])
            for s in range(SLOTS):
                link(g.tensor_scalar(lt[:, s], iota_e[:], rt[:, 3, s:s + 1], rt[:, 2, s:s + 1],
                                     ALU.is_equal, ALU.mult))
            link(g.tensor_tensor(by_expert[:, 2], lt[:, 0], lt[:, 1], ALU.add))
            link(g.tensor_tensor(by_expert[:, 0], by_expert[:, 2], seg_mask[:, 0], ALU.mult))
            link(g.tensor_tensor(by_expert[:, 1], by_expert[:, 2], seg_mask[:, 1], ALU.mult))
            for b in range(B):
                last = g.tensor_scalar(coef_diag[:, b], coef_row[:], ident2[:, b:b + 1], None, ALU.mult)
            last.then_inc(diag_ready, 1)

            for n in range(1, LOADS):
                if n == 2:
                    pool.wait_ge(norm_sq_ready, 1)
                    g.tensor_tensor(norm[:], norm_sq[:], minus_half[:], ALU.pow).then_inc(norm_ready, 1)
                u = n % 2
                pool.wait_ge(w1_landed, 16 * n)
                if n in LAST_STEP_OF_BUFFER:
                    pool.wait_ge(hidden_ready, HC * LAST_STEP_OF_BUFFER[n])
                src = w1_raw[:].rearrange("p c (m j) -> p c j m", j=HC)
                for c in range(DC):
                    link(g.tensor_copy(w1_hi[:, u, c], src[:, c]))
                    g.tensor_tensor(w1_lo[:, u, c], src[:, c], w1_hi[:, u, c].bitcast(F32), ALU.subtract).then_inc(w1_ready, 1)
                pool.wait_ge(w2_landed, 16 * (n + 1))
                if n in LAST_STEP_OF_BUFFER:
                    pool.wait_ge(h_used, HC * LAST_STEP_OF_BUFFER[n])
                for c in range(2):
                    js = slice(c * HC // 2, (c + 1) * HC // 2)
                    link(g.tensor_copy(w2_hi[:, u, js], w2_raw[:, js]))
                    g.tensor_tensor(w2_lo[:, u, js], w2_raw[:, js], w2_hi[:, u, js].bitcast(F32), ALU.subtract).then_inc(w2_ready, 1)

        @block.scalar
        def _(act):
            w1_src_j = w1_raw[:].rearrange("p c (m j) -> p c j m", j=HC)
            act.wait_ge(ident_ready, 1)
            nc.scalar.activation(table_warm[:], ident[:, 0:1], ACT.Gelu_apprx_tanh)

            def copy_x(grp):
                act.wait_ge(extra_ready, USE[f"x{grp}"] + 1)
                for c in range(DC):
                    nc.scalar.activation(x_hi[:, c, span(grp)], extra[c][:], ACT.Copy)
                    nc.scalar.activation(acc[:, c, span(grp)], extra[c][:], ACT.Copy).then_inc(x_copied, 1)

            def copy_rows(name):
                f = 2 * int(name[1]) + int(name[2])
                for c in range(IC):
                    act.wait_ge(rows_in_psum, IC * f + c + 1)
                    nc.scalar.activation(rows[:, c], extra[c][:], ACT.Copy).then_inc(rows_copied, 1)

            copy_x(0)
            js = slice(HC // 2, HC)
            for c in range(DC):
                act.wait_ge(sw1_landed[c], 16)
                nc.scalar.activation(w1_hi[:, 0, c, js], w1_src_j[:, c, js], ACT.Copy).then_inc(sw_hi_ready, 1)
            act.wait_ge(w2_landed, 16)
            for q in range(2):
                js = slice(q * HC // 2, (q + 1) * HC // 2)
                nc.scalar.activation(w2_hi[:, 0, js], w2_raw[:, js], ACT.Copy).then_inc(sw_hi_ready, 1)

            def extras(names):
                for name in names:
                    if name[0] == "x":
                        copy_x(int(name[1]))
                    elif name[0] == "T":
                        copy_rows(name)

            def add_biases(b, j):
                if j == 0:
                    act.wait_ge(bias_ready, DC)
                    act.wait_ge(acc_ready, DC * 2 * (b + 1))
                parts = [(half, c, *piece) for half in range(2) for c in range(DC) for piece in pieces(half)]
                for half, c, s, r, rs, i0, i1, _ in parts[j * len(parts) // HC:(j + 1) * len(parts) // HC]:
                    to = acc[:, c, span(2 * b + half)].rearrange("p (r i) -> p r i", r=RH)[:, r:r + rs, i0:i1]
                    last = nc.scalar.activation(to, to, ACT.Identity, bias=bias[:, c, b, s:s + 1])
                if j == HC - 1:
                    last.then_inc(biases_added, 1)

            def step(t, kind):
                load = UNITS[t // 2][0]
                cols = slice(0, width(WINDOWS[kind]))
                for j in range(HC):
                    n = HC * t + j
                    act.wait_ge(hidden_ready, n + 1)
                    if n >= G_RING:
                        act.wait_ge(h_ready, n - G_RING + 1)
                    if j == 0:
                        act.wait_ge(b1_landed[load], 16)
                    nc.scalar.activation(gelu[:, n % G_RING, cols], hid[n % HID_RING][:, cols], ACT.Gelu_apprx_tanh,
                                         bias=b1[:, load, j:j + 1]).then_inc(gelu_ready, 1)
                    if t in (3, 5):
                        add_biases((t - 3) // 2, j)
                    extras(hooks(t, j))

            def unit(u, kind=None):
                for half in range(2):
                    step(2 * u + half, kind)

            for u in range(B):
                unit(u)
            experts = load_experts(act)
            for u in range(B, len(UNITS)):
                by_expert_kind(act, experts[u - B], lambda kind: unit(u, kind))
            extras(TAIL)

        @block.vector
        def _(dve):
            chain = [0]

            def link(ins):
                chain[0] += 1
                ins.then_inc(dve_step, 1)
                dve.wait_ge(dve_step, chain[0])

            v = nc.vector

            def sum_tokens(grp):
                b, half = grp // 2, grp % 2
                dve.wait_ge(x_copied, DC * (grp + 1))
                for n, (s, r, rs, i0, i1, _) in enumerate(pieces(half)):
                    run = sum(q[0] == s for q in pieces(half)[:n]) + half * sum(q[0] == s for q in pieces(0))
                    tokens = acc[:, :, span(grp)].rearrange("p c (r i) -> p c r i", r=RH)[:, :, r:r + rs, i0:i1]
                    last = v.tensor_reduce(run_sum[:, s, :, b, run], tokens, mybir.AxisListType.XY, ALU.add)
                if grp == GROUPS - 1:
                    link(last)
                    v.tensor_reduce(seg_sum[:], run_sum[:], AX_X, ALU.add).then_inc(seg_sum_ready, 1)

            def add_step(t, kind=None):
                load, b = UNITS[t // 2]
                half = t % 2
                if t == 0:
                    dve.wait_ge(b2_landed, 16 * (1 + E))
                if load > 0:
                    dve.wait_ge(biases_added, b + 1)
                g0 = (2 * b + half) * HALF
                for c in range(DC):
                    if c < DC - 1:
                        dve.wait_ge(step_ready, t + 1)
                    else:
                        dve.wait_ge(h_used, HC * (t + 1))
                    if load == 0:
                        to = acc[:, c, g0:g0 + HALF]
                        last = v.scalar_tensor_tensor(out=to, in0=mlp[c][:], scalar=sb2_col[:, c:c + 1], in1=to,
                                                      op0=ALU.add, op1=ALU.add)
                        last.then_inc(acc_ready, 1)
                        continue
                    cols = width(WINDOWS[kind])
                    for s, r, rs, i0, i1, at in pieces(half, WINDOWS[kind]):
                        if (kind, s) in ((NOT_HEAD, 0), (NOT_WRIST, 1)):
                            continue
                        to = acc[:, c, g0:g0 + HALF].rearrange("p (r i) -> p r i", r=RH)[:, r:r + rs, i0:i1]
                        of = mlp[c][:, 0:cols].rearrange("p (r i) -> p r i", r=RH)[:, r:r + rs, at:at + i1 - i0]
                        k = (load - 1) % SLOTS * SEG + s
                        last = v.scalar_tensor_tensor(out=to, in0=of, scalar=coef[:, b, k:k + 1], in1=to,
                                                      op0=ALU.mult, op1=ALU.add)
                    last.then_inc(acc_ready, 1)

            def extras(names):
                for name in names:
                    if name[0] == "x":
                        continue
                    if name[:3] == "sum":
                        sum_tokens(int(name[3]))
                        continue
                    if name in ("logits", "coef", "modT", "normsq"):
                        dve.wait_ge(extra_ready, USE[name] + 1)
                    if name == "logits":
                        v.tensor_copy(lg[:], extra[0][0:B, 0:3 * E]).then_inc(logits_ready, 1)
                    elif name == "coef":
                        v.tensor_copy(coef[:].rearrange("p b k -> p (b k)"), extra[0][:, 0:B * COEF]).then_inc(coef_ready, 1)
                        dve.wait_ge(coef_ready, 1)
                        for c in range(DC):
                            link(v.tensor_tensor(bias_t[:], coef[:, :, SLOTS * SEG:].rearrange("p b (g e) -> p b g e", e=E),
                                                 eb2_col[:, c, :].unsqueeze(1).unsqueeze(1).to_broadcast([P, B, SEG, E]), ALU.mult))
                            v.tensor_reduce(bias[:, c], bias_t[:], AX_X, ALU.add).then_inc(bias_ready, 1)
                            dve.wait_ge(bias_ready, c + 1)
                    elif name == "modT":
                        dve.wait_ge(cond_landed, 16 * B)
                        link(v.tensor_scalar(mod_y[:], cond_col[:], float(D) ** -0.5, None, ALU.mult))
                        for b in range(B):
                            for c in range(IC):
                                v.tensor_scalar(mod_t[:, b, c], extra[0][:, c * D:(c + 1) * D], mod_y[:, c, b:b + 1],
                                                None, ALU.mult).then_inc(mod_scaled, 1)
                        dve.wait_ge(mod_scaled, B * IC)
                        v.tensor_tensor(mod_sq[:], mod_t[:], mod_t[:], ALU.mult).then_inc(mod_ready, 1)
                        v.tensor_copy(mod_hi[:], mod_t[:]).then_inc(mod_ready, 1)
                        dve.wait_ge(mod_ready, 2)
                        v.tensor_tensor(mod_lo[:], mod_t[:], mod_hi[:], ALU.subtract).then_inc(mod_ready, 1)
                    elif name == "normsq":
                        v.tensor_scalar(norm_sq[:], extra[0][:, 0:B * DC], EPS_NORM, None, ALU.add).then_inc(norm_sq_ready, 1)
                    elif name[0] == "T":
                        f = 2 * int(name[1]) + int(name[2])
                        for c in range(IC):
                            dve.wait_ge(rows_copied, IC * f + c + 1)
                            link(v.tensor_copy(rows_hi[:, c], rows[:, c]))
                            v.tensor_tensor(rows_lo[:, c], rows[:, c], rows_hi[:, c], ALU.subtract).then_inc(rows_ready, 1)
                    elif name[0] == "M":
                        b, f = int(name[1]), 2 * int(name[1]) + int(name[2])
                        dve.wait_ge(norm_ready, 1)
                        for c in range(DC):
                            dve.wait_ge(conv_ready, DC * f + c + 1)
                            if f > 0:
                                dve.wait_ge(stored, 16 * DC * f)
                            v.scalar_tensor_tensor(out=y[:, c], in0=extra[c][:], scalar=norm[:, b * DC + c:b * DC + c + 1],
                                                   in1=rows[:, c], op0=ALU.mult, op1=ALU.add).then_inc(y_ready, 1)

            link(v.memset(run_sum[:], 0.0))
            w1_src_j = w1_raw[:].rearrange("p c (m j) -> p c j m", j=HC)

            def split_first_w1(c):
                js = slice(0, HC // 2)
                dve.wait_ge(sw1_landed[c], 16)
                link(v.tensor_copy(w1_hi[:, 0, c, js], w1_src_j[:, c, js]))
                v.tensor_tensor(w1_lo[:, 0, c, js], w1_src_j[:, c, js], w1_hi[:, 0, c, js],
                                ALU.subtract).then_inc(w1_ready, 1)

            def low_first_x(c):
                dve.wait_ge(x_copied, c + 1)
                v.tensor_tensor(x_lo[:, c, span(0)], acc[:, c, span(0)], x_hi[:, c, span(0)],
                                ALU.subtract).then_inc(x_ready[0], 1)

            split_first_w1(0)
            for c in range(DC):
                low_first_x(c)
            split_first_w1(1)
            js = slice(HC // 2, HC)
            for c in range(DC):
                dve.wait_ge(sw_hi_ready, c + 1)
                v.tensor_tensor(w1_lo[:, 0, c, js], w1_src_j[:, c, js], w1_hi[:, 0, c, js],
                                ALU.subtract).then_inc(w1_ready, 1)
            for q in range(2):
                js = slice(q * HC // 2, (q + 1) * HC // 2)
                dve.wait_ge(sw_hi_ready, DC + q + 1)
                v.tensor_tensor(w2_lo[:, 0, js], w2_raw[:, js], w2_hi[:, 0, js], ALU.subtract).then_inc(w2_ready, 1)

            def step(t, kind):
                cols = slice(0, width(WINDOWS[kind]))
                for j in range(HC):
                    n = HC * t + j
                    if n >= H_RING:
                        dve.wait_ge(h_used, n - H_RING + 1)
                    dve.wait_ge(gelu_ready, n + 1)
                    v.tensor_copy(h_hi[:, n % H_RING, cols], gelu[:, n % G_RING, cols]).then_inc(h_hi_ready, 1)
                    dve.wait_ge(h_hi_ready, n + 1)
                    v.tensor_tensor(h_lo[:, n % H_RING, cols], gelu[:, n % G_RING, cols], h_hi[:, n % H_RING, cols],
                                    ALU.subtract).then_inc(h_ready, 1)
                    extras(hooks(t, j))
                    if (t, j) == (0, 3):
                        dve.wait_ge(silu_exp_ready, 1)
                        link(v.tensor_scalar(silu_t[:], silu_e[:], 1.0, None, ALU.add))
                        link(v.reciprocal(silu_e[:], silu_t[:]))
                        v.tensor_tensor(silu[:], silu_e[:], cond_col[:], ALU.mult).then_inc(silu_ready, 1)
                    if (t, j) == (0, HC - 1):
                        dve.wait_ge(prob_ready, 1)
                        v.max(top[:], prob[:]).then_inc(dve_step, 1)
                        chain[0] += 1
                        dve.wait_ge(dve_step, chain[0])
                        v.max_index(top_i[:], top[:], prob[:]).then_inc(top_ready, 1)
                add_step(t, kind)

            def unit(u, kind=None):
                chain[0] = links[u]
                for half in range(2):
                    step(2 * u + half, kind)
                links[u + 1] = chain[0]

            links = {0: chain[0]}
            for u in range(B):
                unit(u)
            experts = load_experts(dve)
            for u in range(B, len(UNITS)):
                by_expert_kind(dve, experts[u - B], lambda kind: unit(u, kind))
            extras(TAIL)

        @block.tensor
        def _(pe):
            def product(to, pairs, first=True, final=True):
                last = len(pairs) - 1
                for k, ((s_hi, s_lo), (m_hi, m_lo)) in enumerate(pairs):
                    nc.tensor.matmul(to, s_hi, m_hi, start=(first and k == 0), stop=False)
                    nc.tensor.matmul(to, s_hi, m_lo, start=False, stop=False)
                    ins = nc.tensor.matmul(to, s_lo, m_hi, start=False, stop=(final and k == last))
                return ins

            def free_extra(name):
                k = USE[name]
                if k == 0:
                    return
                was = USES[k - 1]
                if was[0] == "x":
                    pe.wait_ge(x_copied, DC * (int(was[1]) + 1))
                elif was[0] == "T":
                    pe.wait_ge(rows_copied, IC * (2 * int(was[1]) + int(was[2]) + 1))
                elif was[0] == "M":
                    pe.wait_ge(y_ready, DC * (2 * int(was[1]) + int(was[2]) + 1))
                elif was == "modT":
                    pe.wait_ge(mod_scaled, B * IC)
                else:
                    pe.wait_ge({"logits": logits_ready, "coef": coef_ready,
                                "normsq": norm_sq_ready}[was], 1)

            def extras(names):
                for name in names:
                    if name[:3] == "sum":
                        continue
                    free_extra(name)
                    if name[0] == "x":
                        grp = int(name[1])
                        pe.wait_ge(x_landed[grp], 16)
                        for c in range(DC):
                            for r in range(RH):
                                for i in range(IC):
                                    k = (r * IC + i) * P
                                    last = nc.tensor.transpose(extra[c][:, k:k + P],
                                                               x_raw[:, grp // 2, grp % 2, i, r * D + c * P:r * D + (c + 1) * P], ident[:])
                    elif name == "logits":
                        pe.wait_ge(seg_sum_ready, 1)
                        pe.wait_ge(seg_w_ready, 1)
                        pe.wait_ge(silu_ready, 1)
                        for a in range(SEG):
                            for c in range(DC):
                                nc.tensor.matmul(extra[0][0:B, 0:E], seg_sum[:, a, c], seg_w[:, a, c],
                                                 start=(a + c == 0), stop=(a == SEG - 1 and c == DC - 1))
                        for c in range(DC):
                            last = nc.tensor.matmul(extra[0][0:B, E:3 * E], silu[:, c], time_w_sb[:, c],
                                                    start=(c == 0), stop=(c == DC - 1))
                    elif name == "coef":
                        pe.wait_ge(diag_ready, 1)
                        last = nc.tensor.matmul(extra[0][:, 0:B * COEF], ones[0:B, :],
                                                coef_diag[:].rearrange("b c k -> b (c k)"), start=True, stop=True)
                    elif name == "modT":
                        pe.wait_ge(mod_landed, 16)
                        for i in range(IC):
                            for o in range(DC):
                                k = i * D + o * P
                                last = nc.tensor.transpose(extra[0][:, k:k + P], mod_raw[:, o, i * P:(i + 1) * P], ident[:])
                    elif name == "normsq":
                        pe.wait_ge(mod_ready, 1)
                        for b in range(B):
                            for o in range(DC):
                                k = b * DC + o
                                for i in range(IC):
                                    last = nc.tensor.matmul(extra[0][:, k:k + 1], mod_sq[:, b, i, o * P:(o + 1) * P],
                                                            ones[:, 0:1], start=(i == 0), stop=(i == IC - 1))
                    elif name[0] == "T":
                        b, f = int(name[1]), int(name[2])
                        t = 2 * (SLOTS * b + SLOTS + B - 1) + f
                        for c in range(DC):
                            pe.wait_ge(acc_ready, DC * t + c + 1)
                            for i in range(IC):
                                for r in range(RH):
                                    k = (2 * b + f) * HALF + r * D + i * P
                                    last = nc.tensor.transpose(extra[i][:, r * D + c * P:r * D + (c + 1) * P],
                                                               acc[:, c, k:k + P], ident[:])
                                if c == DC - 1:
                                    last.then_inc(rows_in_psum, 1)
                        continue
                    elif name[0] == "M":
                        b, f = int(name[1]), int(name[2])
                        pe.wait_ge(mod_ready, 3)
                        for i in range(IC):
                            pe.wait_ge(rows_ready, IC * (2 * b + f) + i + 1)
                            for o in range(DC):
                                os = slice(o * P, (o + 1) * P)
                                last = product(extra[o][:], [((mod_hi[:, b, i, os], mod_lo[:, b, i, os]), (rows_hi[:, i], rows_lo[:, i]))],
                                               first=(i == 0), final=(i == IC - 1))
                                if i == IC - 1:
                                    last.then_inc(conv_ready, 1)
                        continue
                    last.then_inc(extra_ready, 1)

            pe.wait_ge(ident_ready, 1)
            extras(["x0"])
            def step(t, kind):
                load, b = UNITS[t // 2]
                grp = 2 * b + t % 2
                u = load % 2
                cols = slice(0, width(WINDOWS[kind]))

                def first(j):
                    n = HC * t + j
                    if j == 0 and t > 0:
                        pe.wait_ge(x_ready[grp], DC)
                    if load and j == 0:
                        pe.wait_ge(w1_ready, 2 * DC + 2 * load)
                    if n >= HID_RING:
                        pe.wait_ge(gelu_ready, n - HID_RING + 1)
                    for c in range(DC):
                        if t == 0 and j % (HC // 2) == 0:
                            pe.wait_ge(x_ready[grp], c + 1)
                            pe.wait_ge(w1_ready, j // (HC // 2) * DC + c + 1)
                        moving = tuple(columns(x, c, grp, WINDOWS[kind]) for x in (x_hi, x_lo))
                        last = product(hid[n % HID_RING][:, cols], [((w1_hi[:, u, c, j], w1_lo[:, u, c, j]), moving)],
                                       first=(c == 0), final=(c == DC - 1))
                    last.then_inc(hidden_ready, 1)

                def second(j, c):
                    n = HC * t + j
                    if t == 0 and j % (HC // 2) == 0:
                        pe.wait_ge(w2_ready, 1 + j // (HC // 2))
                    elif load and j == 0:
                        pe.wait_ge(w2_ready, 2 * (load + 1))
                    if j == 0 and t > 0:
                        pe.wait_ge(acc_ready, DC * (t - 1) + c + 1)
                    pe.wait_ge(h_ready, n + 1)
                    q = n % H_RING
                    cs = slice(c * P, (c + 1) * P)
                    last = product(mlp[c][:, cols], [((w2_hi[:, u, j, cs], w2_lo[:, u, j, cs]), (h_hi[:, q, cols], h_lo[:, q, cols]))],
                                   first=(j == 0), final=(j == HC - 1))
                    if c == DC - 1:
                        last.then_inc(h_used, 1)
                    elif j == HC - 1:
                        last.then_inc(step_ready, 1)

                for j in range(HC):
                    first(j)
                    extras(hooks(t, j))
                    if j >= LAG:
                        for c in range(DC):
                            second(j - LAG, c)
                for c in range(DC):
                    for j in range(HC - LAG, HC):
                        second(j, c)

            def unit(u, kind=None):
                for half in range(2):
                    step(2 * u + half, kind)

            for u in range(B):
                unit(u)
            experts = load_experts(pe)
            for u in range(B, len(UNITS)):
                by_expert_kind(pe, experts[u - B], lambda kind: unit(u, kind))
            extras(TAIL)


_INS = ['x', 'cond_1024', 'L0_cond_gate_w', 'L0_cond_gate_b', 'L0_cond_time_w', 'L0_cond_time_b',
        'L0_cond_ew1', 'L0_cond_eb1', 'L0_cond_ew2', 'L0_cond_eb2', 'L0_cond_sw1', 'L0_cond_sb1',
        'L0_cond_sw2', 'L0_cond_sb2', 'L1_cond_weight']
_OUTS = [((2, 1024, 256), 'float32')]


def kernel(**inputs):
    import numpy as _np
    import concourse.bacc as _bacc
    from concourse import mybir as _mybir
    from concourse.bass_utils import run_bass_kernel_spmd as _run

    nc = _bacc.Bacc("TRN2", target_bir_lowering=False, num_devices=1)
    arrays, args = {}, []
    for name in _INS:
        a = _np.ascontiguousarray(inputs[name])
        arrays[f"in_{name}_dram"] = a
        args.append(nc.dram_tensor(f"in_{name}_dram", a.shape, _mybir.dt.from_np(a.dtype), kind="ExternalInput").ap())
    for i, (shape, dtype) in enumerate(_OUTS):
        dt = _mybir.dt.from_np(_np.dtype(dtype))
        args.append(nc.dram_tensor(f"out_{i}_dram", shape, dt, kind="ExternalOutput").ap())
    build(nc, *args)
    r = _run(nc, [arrays], core_ids=[0])
    return r.results[0]["out_0_dram"]
```

```python
from contextlib import ExitStack

import concourse.bass as bass
from concourse import mybir

F32 = mybir.dt.float32
F32R = mybir.dt.float32r
U32 = mybir.dt.uint32
ALU = mybir.AluOpType
ACT = mybir.ActivationFunctionType
AX_X = mybir.AxisListType.X

P = 128
EULER = 2.718281828459045
EPS_TOPK = 1e-08
EPS_NORM = 1e-08


def build(nc, x, cond, gate_w, gate_b, time_w, time_b, ew1, eb1, ew2, eb2, sw1, sb1, sw2, sb2, mod_w, out):
    B, L, D = x.shape
    E = gate_w.shape[1]
    H = sw1.shape[1]
    R = L // D
    RH = R // 2
    DC = D // P
    IC = D // P
    HC = H // P
    HALF = RH * D
    SLOTS = 2
    SEG = 3
    HEAD = L // 3
    WRIST = 2 * (L // 3)
    NOT_WRIST, NOT_HEAD = 1, 2
    GROUPS = 2 * B
    COEF = SLOTS * SEG + SEG * E
    AGG = 3
    assert HALF == 512 and B == 2 and E == 4 and DC == 2 and R == 4

    LOADS = 1 + B * SLOTS
    UNITS = [(0, b) for b in range(B)] + [(1 + b * SLOTS + s, b) for b in range(B) for s in range(SLOTS)]
    STEPS = [(u, r, RH) for u in range(len(UNITS)) for r in (0, RH)]
    PARTS = [(UNITS[u][1], r, n, t) for t, (u, r, n) in enumerate(STEPS)
             if u == len(UNITS) - 1 or (UNITS[u][0] and UNITS[u][1] != UNITS[u + 1][1])]
    PARTS[-1:] = [(B - 1, r, 1, len(STEPS) - 1) for r in range(RH, R)]

    H_RING, HID_RING, G_RING = 4, 4, 3
    WARM_UPS = 5, 8
    LAG = 3

    USES = ["x0", "x1", "x2", "x3", "logits", "coef", "modT", "normsq",
            "T0", "M0", "T1", "M1", "T2", "M2", "T3"]
    USE = {name: n for n, name in enumerate(USES)}

    head_i, wrist_i = -(-HEAD // R), WRIST // R
    from_i = HEAD // R - (D - HEAD // R) % 2
    ALL = [(0, D)]
    WINDOWS = {None: ALL, NOT_WRIST: [(0, head_i), (wrist_i, D)], NOT_HEAD: [(from_i, D)]}
    assert head_i == D - wrist_i and head_i % 2 == 0

    def width(rs, windows):
        return rs * sum(b - a for a, b in windows)

    def pieces(r0, rs, windows=ALL):
        found = []
        for s in range(SEG):
            by_r = []
            for r in range(r0, r0 + rs):
                ends = [0, -(-(HEAD - r) // R), -(-(WRIST - r) // R), D]
                row, at = [], 0
                for a, b in windows:
                    i0, i1 = max(a, ends[s]), min(b, ends[s + 1])
                    if i0 < i1:
                        row.append((i0, i1, at + i0 - a))
                    at += b - a
                by_r.append(row)
            if all(row == by_r[0] for row in by_r):
                found += [(s, 0, rs, *run) for run in by_r[0]]
            else:
                found += [(s, r, 1, *run) for r, row in enumerate(by_r) for run in row]
        return found

    with ExitStack() as ctx:
        def sb(name, shape, dt=F32):
            return ctx.enter_context(nc.sbuf_tensor(name, shape, dt))

        def sem(name):
            return ctx.enter_context(nc.semaphore(name))

        x_raw = sb("x_raw", [P, B, 2, IC, HALF])
        acc = sb("acc", [P, DC, GROUPS * HALF])
        x_hi = sb("x_hi", [P, DC, GROUPS * HALF], F32R)
        x_lo = sb("x_lo", [P, DC, GROUPS * HALF], F32R)
        gelu = sb("gelu", [P, G_RING, HALF])
        h_hi = sb("h_hi", [P, H_RING, HALF], F32R)
        h_lo = sb("h_lo", [P, H_RING, HALF], F32R)
        w1_raw = sb("w1_raw", [P, DC, H])
        w2_raw = sb("w2_raw", [P, HC, D])
        w1_hi = sb("w1_hi", [P, 2, DC, HC, P], F32R)
        w1_lo = sb("w1_lo", [P, 2, DC, HC, P], F32R)
        w2_hi = sb("w2_hi", [P, 2, HC, D], F32R)
        w2_lo = sb("w2_lo", [P, 2, HC, D], F32R)
        b1 = sb("b1", [P, LOADS, HC])
        eb2_col = sb("eb2_col", [P, DC, E])
        sb2_col = sb("sb2_col", [P, DC])
        RUNS = 3
        run_sum = sb("run_sum", [P, SEG, DC, B, RUNS])
        seg_sum = sb("seg_sum", [P, SEG, DC, B])
        avg_w = sb("avg_w", [P, AGG, DC, E])
        seg_w = sb("seg_w", [P, SEG, DC, E])
        gate_w_sb = sb("gate_w_sb", [P, AGG, DC, E])
        time_w_sb = sb("time_w_sb", [P, DC, 2 * E])
        gate_b_sb = sb("gate_b_sb", [B, E])
        time_b_sb = sb("time_b_sb", [B, 2 * E])
        cond_col = sb("cond_col", [P, DC, B])
        silu_t = sb("silu_t", [P, DC, B])
        silu_e = sb("silu_e", [P, DC, B])
        silu = sb("silu", [P, DC, B])
        base_e = sb("base_e", [P, E])
        lg = sb("lg", [B, 3 * E])
        lt = sb("lt", [B, 8, E])
        prob = sb("prob", [B, 8])
        top = sb("top", [B, 8])
        top_i = sb("top_i", [B, 8], U32)
        rt = sb("rt", [B, 8, SLOTS])
        ident2 = sb("ident2", [B, B])
        iota_e = sb("iota_e", [B, E])
        seg_mask = sb("seg_mask", [B, 2, E])
        coef_row = sb("coef_row", [B, COEF])
        coef_diag = sb("coef_diag", [B, B, COEF])
        coef = sb("coef", [P, B, COEF])
        bias_t = sb("bias_t", [P, B, SEG, E])
        bias = sb("bias", [P, DC, B, SEG])
        mod_raw = sb("mod_raw", [P, DC, D])
        mod_y = sb("mod_y", [P, IC, B])
        mod_t = sb("mod_t", [P, B, IC, D])
        mod_hi = sb("mod_hi", [P, B, IC, D], F32R)
        mod_lo = sb("mod_lo", [P, B, IC, D], F32R)
        mod_sq = sb("mod_sq", [P, B, IC, D])
        norm_sq = sb("norm_sq", [P, B * DC])
        minus_half = sb("minus_half", [P, B * DC])
        minus_one = sb("minus_one", [B, 1])
        norm = sb("norm", [P, B * DC])
        rows = sb("rows", [P, IC, HALF])
        rows_hi = sb("rows_hi", [P, IC, HALF], F32R)
        rows_lo = sb("rows_lo", [P, IC, HALF], F32R)
        y = sb("y", [P, DC, HALF])
        ident = sb("ident", [P, P])
        table_warm = sb("table_warm", [P, 1])
        ones = sb("ones", [P, P])

        hid = [ctx.enter_context(nc.psum_tensor(f"hid{n}", [P, HALF], F32)) for n in range(HID_RING)]
        mlp = [ctx.enter_context(nc.psum_tensor(f"mlp{n}", [P, HALF], F32)) for n in range(DC)]
        extra = [ctx.enter_context(nc.psum_tensor(f"extra{n}", [P, HALF], F32)) for n in range(2)]

        x_landed = [sem(f"x_landed{g}") for g in range(GROUPS)]
        w1_landed = sem("w1_landed")
        w2_landed = sem("w2_landed")
        b1_landed = [sem(f"b1_landed{n}") for n in range(LOADS)]
        cond_landed = sem("cond_landed")
        router_landed = sem("router_landed")
        b2_landed = sem("b2_landed")
        mod_landed = sem("mod_landed")
        pool_step = sem("pool_step")
        dve_step = sem("dve_step")
        consts_ready = sem("consts_ready")
        silu_exp_ready = sem("silu_exp_ready")
        silu_ready = sem("silu_ready")
        sw_hi_ready = sem("sw_hi_ready")
        w_hi_ready = sem("w_hi_ready")
        w1_ready = sem("w1_ready")
        w2_ready = sem("w2_ready")
        x_copied = sem("x_copied")
        x_ready = [sem(f"x_ready{g}") for g in range(GROUPS)]
        sw1_landed = [sem(f"sw1_landed{c}") for c in range(DC)]
        ident_ready = sem("ident_ready")
        seg_w_ready = sem("seg_w_ready")
        seg_sum_ready = sem("seg_sum_ready")
        rows_in_psum = sem("rows_in_psum")
        conv_ready = sem("conv_ready")
        hidden_ready = sem("hidden_ready")
        gelu_ready = sem("gelu_ready")
        h_hi_ready = sem("h_hi_ready")
        h_ready = sem("h_ready")
        step_ready = sem("step_ready")
        h_used = sem("h_used")
        acc_ready = sem("acc_ready")
        extra_ready = sem("extra_ready")
        coef_ready = sem("coef_ready")
        bias_ready = sem("bias_ready")
        biases_added = sem("biases_added")
        mod_scaled = sem("mod_scaled")
        logits_ready = sem("logits_ready")
        prob_ready = sem("prob_ready")
        top_ready = sem("top_ready")
        diag_ready = sem("diag_ready")
        mod_ready = sem("mod_ready")
        norm_sq_ready = sem("norm_sq_ready")
        norm_ready = sem("norm_ready")
        x_hi_ready = sem("x_hi_ready")
        rows_hi_ready = sem("rows_hi_ready")
        rows_copied = sem("rows_copied")
        rows_ready = sem("rows_ready")
        y_ready = sem("y_ready")
        stored = sem("stored")

        block = ctx.enter_context(nc.Block())

        LAST_STEP_OF_BUFFER = {2: 4, 3: 6, 4: 8}
        HIGH_FROM = {1: 2 * HC + HC // 2, 2: 4 * HC, 3: 6 * HC, 4: 8 * HC}

        def hooks(t, j):
            return {(0, 0): ["x1", "sum0"], (0, 4): ["x2", "sum1"], (0, 5): ["sum2"], (0, 6): ["x3"],
                    (0, 7): ["sum3"], (1, 1): ["logits"], (1, 3): ["top"], (1, 7): ["coef"],
                    (3, 2): ["modT"], (3, 6): ["normsq"],
                    (7, 2): ["T0"], (7, 6): ["M0"], (8, 2): ["T1"], (8, 6): ["M1"],
                    (11, 2): ["T2"], (11, 6): ["M2"]}.get((t, j), [])

        TAIL = ["T3", "T4", "M3", "M4"]

        def span(b, r, rs):
            return slice((b * R + r) * D, (b * R + r + rs) * D)

        def half_of(g):
            return span(g // 2, g % 2 * RH, RH)

        def columns(tile, c, b, r, rs, windows):
            whole = tile[:, c, span(b, r, rs)]
            if len(windows) == 2:
                (_, a), (b, _) = windows
                return bass.AP(whole.tensor, whole.offset, [list(whole.ap[0]), [D, rs], [b, 2], [1, a]])
            (a, b), = windows
            return whole.rearrange("p (r i) -> p r i", r=rs)[:, :, a:b]

        def rows_bank(k, c):
            return hid[2 + c] if k == len(PARTS) - 1 else extra[c]

        def conv_bank(k, c):
            return {len(PARTS) - 2: hid, len(PARTS) - 1: mlp}.get(k, extra)[c]

        def in_rows(r, rs):
            return slice(r % RH * D, (r % RH + rs) * D)

        def load_experts(eng):
            eng.wait_ge(top_ready, 1)
            return [eng.value_load(top_i[b:b + 1, s:s + 1], min_val=0, max_val=E - 1)
                    for b in range(B) for s in range(SLOTS)]

        def by_expert_kind(eng, expert, body):
            with eng.If(expert == NOT_WRIST):
                body(NOT_WRIST)
            with eng.Else():
                with eng.If(expert == NOT_HEAD):
                    body(NOT_HEAD)
                with eng.Else():
                    body(None)
                eng.nop()

        w1_src = [sw1.rearrange("(c p) h -> p c h", p=P), ew1.rearrange("e (c p) h -> e p c h", p=P)]
        w2_src = [sw2.rearrange("(p j) d -> p j d", j=HC), ew2.rearrange("e (p j) d -> e p j d", j=HC)]
        b1_src = [sb1.rearrange("(p j) -> p j", j=HC), eb1.rearrange("e (p j) -> e p j", j=HC)]
        x_src = x.rearrange("b (c p f r) d -> b f p c (r d)", p=P, f=2, r=RH)
        out_dst = out.rearrange("b (c p r) d -> b p c (r d)", p=P, r=R)

        @block.sync
        def _(sp):
            def load_x(g):
                sp.dma_start(x_raw[:, g // 2, g % 2], x_src[g // 2, g % 2]).then_inc(x_landed[g], 16)

            load_x(0)
            for c in range(DC):
                sp.dma_start(w1_raw[:, c], w1_src[0][:, c]).then_inc(sw1_landed[c], 16)
            sp.dma_start(b1[:, 0, :], b1_src[0]).then_inc(b1_landed[0], 16)
            load_x(1)
            sp.dma_start(w2_raw[:], w2_src[0]).then_inc(w2_landed, 16)
            for g in range(2, GROUPS):
                load_x(g)
            with nc.allow_non_contiguous_dma(reason="a few hundred numbers, onto partitions"):
                for b in range(B):
                    sp.dma_start(cond_col[:, :, b], cond[b].rearrange("(c p) -> p c", p=P)).then_inc(cond_landed, 16)
                sp.dma_start(gate_w_sb[:], gate_w.rearrange("(a c p) e -> p a c e", a=AGG, p=P)).then_inc(router_landed, 16)
                sp.dma_start(time_w_sb[:], time_w.rearrange("(c p) e -> p c e", p=P)).then_inc(router_landed, 16)
                sp.dma_start(gate_b_sb[:], gate_b.rearrange("(a e) -> a e", a=1).to_broadcast([B, E])).then_inc(router_landed, 16)
                sp.dma_start(time_b_sb[:], time_b.rearrange("(a e) -> a e", a=1).to_broadcast([B, 2 * E])).then_inc(router_landed, 16)
                sp.dma_start(sb2_col[:], sb2.rearrange("(c p) -> p c", p=P)).then_inc(b2_landed, 16)
                for e in range(E):
                    sp.dma_start(eb2_col[:, :, e], eb2[e].rearrange("(c p) -> p c", p=P)).then_inc(b2_landed, 16)
            sp.dma_start(mod_raw[:], mod_w[0, :, :, 0].rearrange("(c p) i -> p c i", p=P)).then_inc(mod_landed, 16)
            experts = load_experts(sp)
            for n in range(1, LOADS):
                e = experts[n - 1]
                sp.dma_start(b1[:, n, :], b1_src[1][bass.ds(e, 1)].rearrange("e p j -> p (e j)")).then_inc(b1_landed[n], 16)
                sp.wait_ge(w1_ready, 2 * DC + 2 * (n - 1))
                sp.dma_start(w1_raw[:], w1_src[1][bass.ds(e, 1)].rearrange("e p c h -> p (e c) h")).then_inc(w1_landed, 16)
                sp.wait_ge(w2_ready, 2 * n)
                sp.dma_start(w2_raw[:], w2_src[1][bass.ds(e, 1)].rearrange("e p j d -> p (e j) d")).then_inc(w2_landed, 16)
            for k, (b, r, rs, _) in enumerate(PARTS):
                for oc in range(DC):
                    sp.wait_ge(y_ready, DC * k + oc + 1)
                    sp.dma_start(out_dst[b, :, oc, r * D:(r + rs) * D], y[:, oc, in_rows(r, rs)]).then_inc(stored, 16)
            sp.wait_ge(stored, 16 * DC * len(PARTS))

        @block.gpsimd
        def _(pool):
            chain = [0]

            def link(ins):
                chain[0] += 1
                ins.then_inc(pool_step, 1)
                pool.wait_ge(pool_step, chain[0])

            g = nc.gpsimd
            link(g.memset(ident[:], 0.0))
            g.affine_select(out=ident[:], in_=ident[:], compare_op=ALU.not_equal, fill=1.0, base=0,
                            pattern=[[-1, P]], channel_multiplier=1).then_inc(ident_ready, 1)
            pool.wait_ge(ident_ready, 1)
            g.memset(ones[:], 1.0)
            g.tensor_copy(ident2[:], ident[0:B, 0:B])
            g.memset(base_e[:], EULER)
            g.memset(minus_half[:], -0.5)
            g.memset(minus_one[:], -1.0)
            for e in range(E):
                g.memset(iota_e[:, e:e + 1], float(e))
            link(g.memset(seg_mask[:], 1.0))
            g.memset(seg_mask[:, 0, NOT_HEAD:NOT_HEAD + 1], 0.0)
            g.memset(seg_mask[:, 1, NOT_WRIST:NOT_WRIST + 1], 0.0)
            g.memset(prob[:], -1.0).then_inc(consts_ready, 1)
            pool.wait_ge(consts_ready, 1)
            pool.wait_ge(cond_landed, 16 * B)
            link(g.tensor_scalar(silu_t[:], cond_col[:], -1.0, None, ALU.mult))
            flat = "p c b -> p (c b)"
            g.tensor_tensor(silu_e[:].rearrange(flat), base_e[:, 0:DC * B], silu_t[:].rearrange(flat),
                            ALU.pow).then_inc(silu_exp_ready, 1)

            pool.wait_ge(router_landed, 64)
            for a, tokens in enumerate((L, L - (WRIST - HEAD), L - HEAD)):
                last = g.tensor_scalar(avg_w[:, a], gate_w_sb[:, a], 1.0 / tokens, None, ALU.mult)
            link(last)
            link(g.tensor_tensor(seg_w[:, 0], avg_w[:, 0], avg_w[:, 1], ALU.add))
            g.tensor_tensor(seg_w[:, 1], avg_w[:, 0], avg_w[:, 2], ALU.add)
            g.tensor_tensor(seg_w[:, 2], seg_w[:, 0], avg_w[:, 2], ALU.add).then_inc(seg_w_ready, 1)
            for grp in range(1, GROUPS):
                pool.wait_ge(x_copied, DC * (grp + 1))
                for c in range(DC):
                    g.tensor_tensor(x_lo[:, c, half_of(grp)], acc[:, c, half_of(grp)], x_hi[:, c, half_of(grp)],
                                    ALU.subtract).then_inc(x_ready[grp], 1)
            pool.wait_ge(logits_ready, 1)
            link(g.tensor_tensor(lt[:, 0], lg[:, 0:E], gate_b_sb[:], ALU.add))
            link(g.tensor_tensor(lt[:, 1:3], lg[:, E:3 * E].rearrange("b (a e) -> b a e", a=2),
                                 time_b_sb[:].rearrange("b (a e) -> b a e", a=2), ALU.add))
            link(g.tensor_scalar(lt[:, 3], lt[:, 1], 1.0, None, ALU.add))
            link(g.tensor_tensor(lt[:, 4], lt[:, 0], lt[:, 3], ALU.mult))
            link(g.tensor_tensor(lt[:, 4], lt[:, 4], lt[:, 2], ALU.add))
            link(g.tensor_scalar(rt[:, 0, 0:1], lt[:, 4, 0:1], lt[:, 4, 1:2], lt[:, 4, 2:3], ALU.max, ALU.max))
            link(g.tensor_scalar(rt[:, 0, 0:1], rt[:, 0, 0:1], lt[:, 4, 3:4], None, ALU.max))
            link(g.tensor_scalar(lt[:, 5], lt[:, 4], rt[:, 0, 0:1], None, ALU.subtract))
            link(g.tensor_tensor(lt[:, 6], base_e[0:B, :], lt[:, 5], ALU.pow))
            link(g.tensor_tensor(rt[:, 7], lt[:, 6, 0:2], lt[:, 6, 2:4], ALU.add))
            link(g.tensor_tensor(rt[:, 0, 1:2], rt[:, 7, 0:1], rt[:, 7, 1:2], ALU.add))
            link(g.tensor_tensor(rt[:, 0, 0:1], rt[:, 0, 1:2], minus_one[:, 0:1], ALU.pow))
            g.tensor_scalar(prob[:, 0:E], lt[:, 6], rt[:, 0, 0:1], None, ALU.mult).then_inc(prob_ready, 1)
            pool.wait_ge(top_ready, 1)
            link(g.tensor_tensor(rt[:, 1, 0:1], top[:, 0:1], top[:, 1:2], ALU.add))
            link(g.tensor_scalar(rt[:, 1, 0:1], rt[:, 1, 0:1], EPS_TOPK, None, ALU.add))
            link(g.tensor_tensor(rt[:, 1, 1:2], rt[:, 1, 0:1], minus_one[:, 0:1], ALU.pow))
            link(g.tensor_scalar(rt[:, 2], top[:, 0:SLOTS], rt[:, 1, 1:2], None, ALU.mult))
            link(g.tensor_copy(rt[:, 3], top_i[:, 0:SLOTS]))
            link(g.tensor_scalar(rt[:, 4], rt[:, 3], float(NOT_HEAD), -1.0, ALU.is_equal, ALU.mult))
            link(g.tensor_scalar(rt[:, 5], rt[:, 3], float(NOT_WRIST), -1.0, ALU.is_equal, ALU.mult))
            link(g.tensor_scalar(rt[:, 4:6], rt[:, 4:6], 1.0, None, ALU.add))
            by_slot = coef_row[:, 0:SLOTS * SEG].rearrange("b (s g) -> b s g", g=SEG)
            by_expert = coef_row[:, SLOTS * SEG:].rearrange("b (g e) -> b g e", e=E)
            g.tensor_tensor(by_slot[:, :, 0], rt[:, 2], rt[:, 4], ALU.mult)
            g.tensor_tensor(by_slot[:, :, 1], rt[:, 2], rt[:, 5], ALU.mult)
            g.tensor_copy(by_slot[:, :, 2], rt[:, 2])
            for s in range(SLOTS):
                link(g.tensor_scalar(lt[:, s], iota_e[:], rt[:, 3, s:s + 1], rt[:, 2, s:s + 1],
                                     ALU.is_equal, ALU.mult))
            link(g.tensor_tensor(by_expert[:, 2], lt[:, 0], lt[:, 1], ALU.add))
            link(g.tensor_tensor(by_expert[:, 0], by_expert[:, 2], seg_mask[:, 0], ALU.mult))
            link(g.tensor_tensor(by_expert[:, 1], by_expert[:, 2], seg_mask[:, 1], ALU.mult))
            for b in range(B):
                last = g.tensor_scalar(coef_diag[:, b], coef_row[:], ident2[:, b:b + 1], None, ALU.mult)
            last.then_inc(diag_ready, 1)

            for n in range(1, LOADS):
                if n == 2:
                    pool.wait_ge(norm_sq_ready, 1)
                    g.tensor_tensor(norm[:], norm_sq[:], minus_half[:], ALU.pow).then_inc(norm_ready, 1)
                u = n % 2
                w1_src_j = w1_raw[:].rearrange("p c (m j) -> p c j m", j=HC)
                for c in range(DC):
                    pool.wait_ge(w_hi_ready, 4 * (n - 1) + c + 1)
                    g.tensor_tensor(w1_lo[:, u, c], w1_src_j[:, c], w1_hi[:, u, c], ALU.subtract).then_inc(w1_ready, 1)
                for c in range(2):
                    js = slice(c * HC // 2, (c + 1) * HC // 2)
                    pool.wait_ge(w_hi_ready, 4 * (n - 1) + 2 + c + 1)
                    g.tensor_tensor(w2_lo[:, u, js], w2_raw[:, js], w2_hi[:, u, js], ALU.subtract).then_inc(w2_ready, 1)

        @block.scalar
        def _(act):
            w1_src_j = w1_raw[:].rearrange("p c (m j) -> p c j m", j=HC)
            act.wait_ge(ident_ready, 1)
            nc.scalar.activation(table_warm[:], ident[:, 0:1], ACT.Gelu_apprx_tanh)

            def copy_x(grp):
                act.wait_ge(extra_ready, USE[f"x{grp}"] + 1)
                for c in range(DC):
                    nc.scalar.activation(x_hi[:, c, half_of(grp)], extra[c][:], ACT.Copy)
                    nc.scalar.activation(acc[:, c, half_of(grp)], extra[c][:], ACT.Copy).then_inc(x_copied, 1)

            def copy_rows(k):
                _, r, rs, _ = PARTS[k]
                to, of = in_rows(r, rs), slice(0, rs * D)
                for c in range(IC):
                    act.wait_ge(rows_in_psum, IC * k + c + 1)
                    nc.scalar.activation(rows_hi[:, c, to], rows_bank(k, c)[:, of], ACT.Copy).then_inc(rows_hi_ready, 1)
                for c in range(IC):
                    act.wait_ge(rows_ready, IC * k + c + 1)
                    nc.scalar.activation(rows[:, c, to], rows_bank(k, c)[:, of], ACT.Copy).then_inc(rows_copied, 1)

            act.wait_ge(extra_ready, USE["x0"] + 1)
            for c in range(DC):
                nc.scalar.activation(x_hi[:, c, half_of(0)], extra[c][:], ACT.Copy).then_inc(x_hi_ready, 1)
            for c in range(DC):
                act.wait_ge(x_ready[0], c + 1)
                nc.scalar.activation(acc[:, c, half_of(0)], extra[c][:], ACT.Copy).then_inc(x_copied, 1)
            js = slice(HC // 2, HC)
            for c in range(DC):
                act.wait_ge(sw1_landed[c], 16)
                nc.scalar.activation(w1_hi[:, 0, c, js], w1_src_j[:, c, js], ACT.Copy).then_inc(sw_hi_ready, 1)

            def high_first_w2(q):
                act.wait_ge(w2_landed, 16)
                js = slice(q * HC // 2, (q + 1) * HC // 2)
                nc.scalar.activation(w2_hi[:, 0, js], w2_raw[:, js], ACT.Copy).then_inc(sw_hi_ready, 1)

            def extras(names):
                for name in names:
                    if name[0] == "x":
                        copy_x(int(name[1]))
                    elif name[0] == "T":
                        copy_rows(int(name[1]))

            def add_biases(b, j):
                if j == 0:
                    act.wait_ge(bias_ready, DC)
                    act.wait_ge(acc_ready, DC * 2 * (b + 1))
                parts = [(r0, c, *piece) for r0 in (0, RH) for c in range(DC) for piece in pieces(r0, RH)]
                for r0, c, s, r, rs, i0, i1, _ in parts[j * len(parts) // HC:(j + 1) * len(parts) // HC]:
                    to = acc[:, c, span(b, r0 + r, rs)].rearrange("p (r i) -> p r i", r=rs)[:, :, i0:i1]
                    last = nc.scalar.activation(to, to, ACT.Identity, bias=bias[:, c, b, s:s + 1])
                if j == HC - 1:
                    last.then_inc(biases_added, 1)

            def high_weights(n, j):
                u, half = n % 2, slice(j % 2 * HC // 2, (j % 2 + 1) * HC // 2)
                if j < HC // 2:
                    c = j // 2
                    if j == 0:
                        act.wait_ge(w1_landed, 16 * n)
                        if n in LAST_STEP_OF_BUFFER:
                            act.wait_ge(hidden_ready, HC * LAST_STEP_OF_BUFFER[n])
                    last = nc.scalar.activation(w1_hi[:, u, c, half], w1_src_j[:, c, half], ACT.Copy)
                else:
                    q = slice((j - HC // 2) * HC // 4, (j - HC // 2 + 1) * HC // 4)
                    if j == HC // 2:
                        act.wait_ge(w2_landed, 16 * (n + 1))
                        if n in LAST_STEP_OF_BUFFER:
                            act.wait_ge(h_used, HC * LAST_STEP_OF_BUFFER[n])
                    last = nc.scalar.activation(w2_hi[:, u, q], w2_raw[:, q], ACT.Copy)
                if j % 2:
                    last.then_inc(w_hi_ready, 1)

            def step(t, kind):
                u, _, rs = STEPS[t]
                load = UNITS[u][0]
                cols = slice(0, width(rs, WINDOWS[kind]))
                for j in range(HC):
                    n = HC * t + j
                    act.wait_ge(hidden_ready, n + 1)
                    if n >= G_RING:
                        act.wait_ge(h_ready, n - G_RING + 1)
                    if j == 0:
                        act.wait_ge(b1_landed[load], 16)
                    nc.scalar.activation(gelu[:, n % G_RING, cols], hid[n % HID_RING][:, cols], ACT.Gelu_apprx_tanh,
                                         bias=b1[:, load, j:j + 1]).then_inc(gelu_ready, 1)
                    if n < 2:
                        high_first_w2(n)
                    for load_n, chunk in HIGH_FROM.items():
                        if chunk <= n < chunk + HC:
                            high_weights(load_n, n - chunk)
                    if t in (3, 5):
                        add_biases((t - 3) // 2, j)
                    extras(hooks(t, j))

            def unit(u, kind=None):
                for t in (t for t, at in enumerate(STEPS) if at[0] == u):
                    step(t, kind)

            for u in range(B):
                unit(u)
            experts = load_experts(act)
            for u in range(B, len(UNITS)):
                by_expert_kind(act, experts[u - B], lambda kind: unit(u, kind))
            extras(TAIL)

        @block.vector
        def _(dve):
            chain = [0]

            def link(ins):
                chain[0] += 1
                ins.then_inc(dve_step, 1)
                dve.wait_ge(dve_step, chain[0])

            v = nc.vector

            def sum_tokens(grp):
                b, r0 = grp // 2, grp % 2 * RH
                dve.wait_ge(x_copied, DC * (grp + 1))
                for n, (s, r, rs, i0, i1, _) in enumerate(pieces(r0, RH)):
                    run = sum(q[0] == s for q in pieces(r0, RH)[:n]) + grp % 2 * sum(q[0] == s for q in pieces(0, RH))
                    tokens = acc[:, :, half_of(grp)].rearrange("p c (r i) -> p c r i", r=RH)[:, :, r:r + rs, i0:i1]
                    last = v.tensor_reduce(run_sum[:, s, :, b, run], tokens, mybir.AxisListType.XY, ALU.add)
                if grp == GROUPS - 1:
                    link(last)
                    v.tensor_reduce(seg_sum[:], run_sum[:], AX_X, ALU.add).then_inc(seg_sum_ready, 1)

            def add_step(t, kind=None):
                u, r0, n = STEPS[t]
                load, b = UNITS[u]
                if t == 0:
                    dve.wait_ge(b2_landed, 16 * (1 + E))
                if load > 0:
                    dve.wait_ge(biases_added, b + 1)
                for c in range(DC):
                    if c < DC - 1:
                        dve.wait_ge(step_ready, t + 1)
                    else:
                        dve.wait_ge(h_used, HC * (t + 1))
                    if load == 0:
                        to = acc[:, c, span(b, r0, n)]
                        last = v.scalar_tensor_tensor(out=to, in0=mlp[c][:], scalar=sb2_col[:, c:c + 1], in1=to,
                                                      op0=ALU.add, op1=ALU.add)
                        last.then_inc(acc_ready, 1)
                        continue
                    cols = width(n, WINDOWS[kind])
                    for s, r, rs, i0, i1, at in pieces(r0, n, WINDOWS[kind]):
                        if (kind, s) in ((NOT_HEAD, 0), (NOT_WRIST, 1)):
                            continue
                        to = acc[:, c, span(b, r0 + r, rs)].rearrange("p (r i) -> p r i", r=rs)[:, :, i0:i1]
                        of = mlp[c][:, 0:cols].rearrange("p (r i) -> p r i", r=n)[:, r:r + rs, at:at + i1 - i0]
                        k = (load - 1) % SLOTS * SEG + s
                        last = v.scalar_tensor_tensor(out=to, in0=of, scalar=coef[:, b, k:k + 1], in1=to,
                                                      op0=ALU.mult, op1=ALU.add)
                    last.then_inc(acc_ready, 1)

            def extras(names):
                for name in names:
                    if name[0] == "x":
                        continue
                    if name[:3] == "sum":
                        sum_tokens(int(name[3]))
                        continue
                    if name == "top":
                        dve.wait_ge(prob_ready, 1)
                        link(v.max(top[:], prob[:]))
                        v.max_index(top_i[:], top[:], prob[:]).then_inc(top_ready, 1)
                        continue
                    if name in ("logits", "coef", "modT", "normsq"):
                        dve.wait_ge(extra_ready, USE[name] + 1)
                    if name == "logits":
                        v.tensor_copy(lg[:], extra[0][0:B, 0:3 * E]).then_inc(logits_ready, 1)
                    elif name == "coef":
                        v.tensor_copy(coef[:].rearrange("p b k -> p (b k)"), extra[0][:, 0:B * COEF]).then_inc(coef_ready, 1)
                        dve.wait_ge(coef_ready, 1)
                        for c in range(DC):
                            link(v.tensor_tensor(bias_t[:], coef[:, :, SLOTS * SEG:].rearrange("p b (g e) -> p b g e", e=E),
                                                 eb2_col[:, c, :].unsqueeze(1).unsqueeze(1).to_broadcast([P, B, SEG, E]), ALU.mult))
                            v.tensor_reduce(bias[:, c], bias_t[:], AX_X, ALU.add).then_inc(bias_ready, 1)
                            dve.wait_ge(bias_ready, c + 1)
                    elif name == "modT":
                        dve.wait_ge(cond_landed, 16 * B)
                        link(v.tensor_scalar(mod_y[:], cond_col[:], float(D) ** -0.5, None, ALU.mult))
                        for b in range(B):
                            for c in range(IC):
                                v.tensor_scalar(mod_t[:, b, c], extra[0][:, c * D:(c + 1) * D], mod_y[:, c, b:b + 1],
                                                None, ALU.mult).then_inc(mod_scaled, 1)
                        dve.wait_ge(mod_scaled, B * IC)
                        v.tensor_tensor(mod_sq[:], mod_t[:], mod_t[:], ALU.mult).then_inc(mod_ready, 1)
                        v.tensor_copy(mod_hi[:], mod_t[:]).then_inc(mod_ready, 1)
                        dve.wait_ge(mod_ready, 2)
                        v.tensor_tensor(mod_lo[:], mod_t[:], mod_hi[:], ALU.subtract).then_inc(mod_ready, 1)
                    elif name == "normsq":
                        v.tensor_scalar(norm_sq[:], extra[0][:, 0:B * DC], EPS_NORM, None, ALU.add).then_inc(norm_sq_ready, 1)
                    elif name[0] == "T":
                        k = int(name[1])
                        _, r, rs, _ = PARTS[k]
                        for c in range(IC):
                            dve.wait_ge(rows_hi_ready, IC * k + c + 1)
                            v.tensor_tensor(rows_lo[:, c, in_rows(r, rs)], rows_bank(k, c)[:, 0:rs * D], rows_hi[:, c, in_rows(r, rs)],
                                            ALU.subtract).then_inc(rows_ready, 1)
                    elif name[0] == "M":
                        k = int(name[1])
                        b, r, rs, _ = PARTS[k]
                        at = in_rows(r, rs)
                        dve.wait_ge(norm_ready, 1)
                        dve.wait_ge(rows_copied, IC * (k + 1))
                        if k > 0 and r % RH == 0:
                            dve.wait_ge(stored, 16 * DC * k)
                        for c in range(DC):
                            dve.wait_ge(conv_ready, DC * k + c + 1)
                            v.scalar_tensor_tensor(out=y[:, c, at], in0=conv_bank(k, c)[:, 0:rs * D],
                                                   scalar=norm[:, b * DC + c:b * DC + c + 1], in1=rows[:, c, at],
                                                   op0=ALU.mult, op1=ALU.add).then_inc(y_ready, 1)

            link(v.memset(run_sum[:], 0.0))
            w1_src_j = w1_raw[:].rearrange("p c (m j) -> p c j m", j=HC)

            first_js = slice(0, HC // 2)

            def high_first_w1(c):
                dve.wait_ge(sw1_landed[c], 16)
                link(v.tensor_copy(w1_hi[:, 0, c, first_js], w1_src_j[:, c, first_js]))

            def low_first_w1(c):
                v.tensor_tensor(w1_lo[:, 0, c, first_js], w1_src_j[:, c, first_js], w1_hi[:, 0, c, first_js],
                                ALU.subtract).then_inc(w1_ready, 1)

            def low_first_x(c):
                dve.wait_ge(x_hi_ready, c + 1)
                v.tensor_tensor(x_lo[:, c, half_of(0)], extra[c][:], x_hi[:, c, half_of(0)],
                                ALU.subtract).then_inc(x_ready[0], 1)

            high_first_w1(0)
            low_first_w1(0)
            for c in range(DC):
                low_first_x(c)
                if c == 0:
                    high_first_w1(1)
            low_first_w1(1)
            js = slice(HC // 2, HC)
            for c in range(DC):
                dve.wait_ge(sw_hi_ready, c + 1)
                v.tensor_tensor(w1_lo[:, 0, c, js], w1_src_j[:, c, js], w1_hi[:, 0, c, js],
                                ALU.subtract).then_inc(w1_ready, 1)

            def low_first_w2(q):
                js = slice(q * HC // 2, (q + 1) * HC // 2)
                dve.wait_ge(sw_hi_ready, DC + q + 1)
                v.tensor_tensor(w2_lo[:, 0, js], w2_raw[:, js], w2_hi[:, 0, js], ALU.subtract).then_inc(w2_ready, 1)

            def step(t, kind):
                cols = slice(0, width(STEPS[t][2], WINDOWS[kind]))
                for j in range(HC):
                    n = HC * t + j
                    if n >= H_RING:
                        dve.wait_ge(h_used, n - H_RING + 1)
                    dve.wait_ge(gelu_ready, n + 1)
                    v.tensor_copy(h_hi[:, n % H_RING, cols], gelu[:, n % G_RING, cols]).then_inc(h_hi_ready, 1)
                    dve.wait_ge(h_hi_ready, n + 1)
                    v.tensor_tensor(h_lo[:, n % H_RING, cols], gelu[:, n % G_RING, cols], h_hi[:, n % H_RING, cols],
                                    ALU.subtract).then_inc(h_ready, 1)
                    if n < 2:
                        low_first_w2(n)
                    extras(hooks(t, j))
                    if (t, j) == (0, 3):
                        dve.wait_ge(silu_exp_ready, 1)
                        link(v.tensor_scalar(silu_t[:], silu_e[:], 1.0, None, ALU.add))
                        link(v.reciprocal(silu_e[:], silu_t[:]))
                        v.tensor_tensor(silu[:], silu_e[:], cond_col[:], ALU.mult).then_inc(silu_ready, 1)
                add_step(t, kind)

            def unit(u, kind=None):
                chain[0] = links[u]
                for t in (t for t, at in enumerate(STEPS) if at[0] == u):
                    step(t, kind)
                links[u + 1] = chain[0]

            links = {0: chain[0]}
            for u in range(B):
                unit(u)
            experts = load_experts(dve)
            for u in range(B, len(UNITS)):
                by_expert_kind(dve, experts[u - B], lambda kind: unit(u, kind))
            extras(TAIL)

        @block.tensor
        def _(pe):
            def product(to, pairs, first=True, final=True):
                last = len(pairs) - 1
                for k, ((s_hi, s_lo), (m_hi, m_lo)) in enumerate(pairs):
                    nc.tensor.matmul(to, s_hi, m_hi, start=(first and k == 0), stop=False)
                    nc.tensor.matmul(to, s_hi, m_lo, start=False, stop=False)
                    ins = nc.tensor.matmul(to, s_lo, m_hi, start=False, stop=(final and k == last))
                return ins

            def free_extra(name):
                k = USE[name]
                if k == 0:
                    return
                was = USES[k - 1]
                if was[0] == "x":
                    pe.wait_ge(x_copied, DC * (int(was[1]) + 1))
                elif was[0] == "T":
                    pe.wait_ge(rows_copied, IC * (int(was[1]) + 1))
                elif was[0] == "M":
                    pe.wait_ge(y_ready, DC * (int(was[1]) + 1))
                elif was == "modT":
                    pe.wait_ge(mod_scaled, B * IC)
                else:
                    pe.wait_ge({"logits": logits_ready, "coef": coef_ready,
                                "normsq": norm_sq_ready}[was], 1)

            def extras(names):
                for name in names:
                    if name[:3] == "sum" or name == "top":
                        continue
                    if name in USE:
                        free_extra(name)
                    if name[0] == "x":
                        grp = int(name[1])
                        pe.wait_ge(x_landed[grp], 16)
                        for c in range(DC):
                            for r in range(RH):
                                for i in range(IC):
                                    k = (r * IC + i) * P
                                    last = nc.tensor.transpose(extra[c][:, k:k + P],
                                                               x_raw[:, grp // 2, grp % 2, i, r * D + c * P:r * D + (c + 1) * P], ident[:])
                    elif name == "logits":
                        pe.wait_ge(seg_sum_ready, 1)
                        pe.wait_ge(seg_w_ready, 1)
                        pe.wait_ge(silu_ready, 1)
                        for a in range(SEG):
                            for c in range(DC):
                                nc.tensor.matmul(extra[0][0:B, 0:E], seg_sum[:, a, c], seg_w[:, a, c],
                                                 start=(a + c == 0), stop=(a == SEG - 1 and c == DC - 1))
                        for c in range(DC):
                            last = nc.tensor.matmul(extra[0][0:B, E:3 * E], silu[:, c], time_w_sb[:, c],
                                                    start=(c == 0), stop=(c == DC - 1))
                    elif name == "coef":
                        pe.wait_ge(diag_ready, 1)
                        last = nc.tensor.matmul(extra[0][:, 0:B * COEF], ones[0:B, :],
                                                coef_diag[:].rearrange("b c k -> b (c k)"), start=True, stop=True)
                    elif name == "modT":
                        pe.wait_ge(mod_landed, 16)
                        for i in range(IC):
                            for o in range(DC):
                                k = i * D + o * P
                                last = nc.tensor.transpose(extra[0][:, k:k + P], mod_raw[:, o, i * P:(i + 1) * P], ident[:])
                    elif name == "normsq":
                        pe.wait_ge(mod_ready, 1)
                        for b in range(B):
                            for o in range(DC):
                                k = b * DC + o
                                for i in range(IC):
                                    last = nc.tensor.matmul(extra[0][:, k:k + 1], mod_sq[:, b, i, o * P:(o + 1) * P],
                                                            ones[:, 0:1], start=(i == 0), stop=(i == IC - 1))
                    elif name[0] == "T":
                        k = int(name[1])
                        b, r0, rs, t = PARTS[k]
                        for c in range(DC):
                            pe.wait_ge(acc_ready, DC * t + c + 1)
                            for i in range(IC):
                                for r in range(rs):
                                    tokens = span(b, r0 + r, 1).start + i * P
                                    last = nc.tensor.transpose(rows_bank(k, i)[:, r * D + c * P:r * D + (c + 1) * P],
                                                               acc[:, c, tokens:tokens + P], ident[:])
                                if c == DC - 1:
                                    last.then_inc(rows_in_psum, 1)
                        continue
                    elif name[0] == "M":
                        k = int(name[1])
                        b, r, rs, _ = PARTS[k]
                        pe.wait_ge(mod_ready, 3)
                        for i in range(IC):
                            pe.wait_ge(rows_ready, IC * k + i + 1)
                            for o in range(DC):
                                os = slice(o * P, (o + 1) * P)
                                last = product(conv_bank(k, o)[:, 0:rs * D],
                                               [((mod_hi[:, b, i, os], mod_lo[:, b, i, os]),
                                                 (rows_hi[:, i, in_rows(r, rs)], rows_lo[:, i, in_rows(r, rs)]))],
                                               first=(i == 0), final=(i == IC - 1))
                                if i == IC - 1:
                                    last.then_inc(conv_ready, 1)
                        continue
                    last.then_inc(extra_ready, 1)

            def warm_up(count):
                for _ in range(count):
                    nc.tensor.matmul(hid[0][:, 0:P], ident[:], ident[:], start=True, stop=True)

            pe.wait_ge(ident_ready, 1)
            warm_up(WARM_UPS[0])
            extras(["x0"])
            warm_up(WARM_UPS[1])

            def step(t, kind):
                unit_of, r0, rs = STEPS[t]
                load, b = UNITS[unit_of]
                u = load % 2
                cols = slice(0, width(rs, WINDOWS[kind]))

                def first(j):
                    n = HC * t + j
                    if j == 0 and t > 0:
                        pe.wait_ge(x_ready[2 * b + r0 // RH], DC)
                    if load and j == 0:
                        pe.wait_ge(w1_ready, 2 * DC + 2 * load)
                    if n >= HID_RING:
                        pe.wait_ge(gelu_ready, n - HID_RING + 1)
                    for c in range(DC):
                        if t == 0 and j % (HC // 2) == 0:
                            pe.wait_ge(x_ready[0], c + 1)
                            pe.wait_ge(w1_ready, j // (HC // 2) * DC + c + 1)
                        moving = tuple(columns(x, c, b, r0, rs, WINDOWS[kind]) for x in (x_hi, x_lo))
                        last = product(hid[n % HID_RING][:, cols], [((w1_hi[:, u, c, j], w1_lo[:, u, c, j]), moving)],
                                       first=(c == 0), final=(c == DC - 1))
                    last.then_inc(hidden_ready, 1)

                def second(j, c):
                    n = HC * t + j
                    if t == 0 and j % (HC // 2) == 0:
                        pe.wait_ge(w2_ready, 1 + j // (HC // 2))
                    elif load and j == 0:
                        pe.wait_ge(w2_ready, 2 * (load + 1))
                    if j == 0 and t > 0:
                        pe.wait_ge(acc_ready, DC * (t - 1) + c + 1)
                    pe.wait_ge(h_ready, n + 1)
                    q = n % H_RING
                    cs = slice(c * P, (c + 1) * P)
                    last = product(mlp[c][:, cols], [((w2_hi[:, u, j, cs], w2_lo[:, u, j, cs]), (h_hi[:, q, cols], h_lo[:, q, cols]))],
                                   first=(j == 0), final=(j == HC - 1))
                    if c == DC - 1:
                        last.then_inc(h_used, 1)
                    elif j == HC - 1:
                        last.then_inc(step_ready, 1)

                for j in range(HC):
                    first(j)
                    extras(hooks(t, j))
                    if j >= LAG:
                        for c in range(DC):
                            second(j - LAG, c)
                for c in range(DC):
                    for j in range(HC - LAG, HC):
                        second(j, c)

            def unit(u, kind=None):
                for t in (t for t, at in enumerate(STEPS) if at[0] == u):
                    step(t, kind)

            for u in range(B):
                unit(u)
            experts = load_experts(pe)
            for u in range(B, len(UNITS)):
                by_expert_kind(pe, experts[u - B], lambda kind: unit(u, kind))
            extras(TAIL)


_INS = ['x', 'cond_1024', 'L0_cond_gate_w', 'L0_cond_gate_b', 'L0_cond_time_w', 'L0_cond_time_b',
        'L0_cond_ew1', 'L0_cond_eb1', 'L0_cond_ew2', 'L0_cond_eb2', 'L0_cond_sw1', 'L0_cond_sb1',
        'L0_cond_sw2', 'L0_cond_sb2', 'L1_cond_weight']
_OUTS = [((2, 1024, 256), 'float32')]


def kernel(**inputs):
    import numpy as _np
    import concourse.bacc as _bacc
    from concourse import mybir as _mybir
    from concourse.bass_utils import run_bass_kernel_spmd as _run

    nc = _bacc.Bacc("TRN2", target_bir_lowering=False, num_devices=1)
    arrays, args = {}, []
    for name in _INS:
        a = _np.ascontiguousarray(inputs[name])
        arrays[f"in_{name}_dram"] = a
        args.append(nc.dram_tensor(f"in_{name}_dram", a.shape, _mybir.dt.from_np(a.dtype), kind="ExternalInput").ap())
    for i, (shape, dtype) in enumerate(_OUTS):
        dt = _mybir.dt.from_np(_np.dtype(dtype))
        args.append(nc.dram_tensor(f"out_{i}_dram", shape, dt, kind="ExternalOutput").ap())
    build(nc, *args)
    r = _run(nc, [arrays], core_ids=[0])
    return r.results[0]["out_0_dram"]
```
